# Optimizing a Trainium2 kernel written in Bass

```python
import numpy as np
import jax
import jax.numpy as jnp

def _softmax(x, axis=-1):
    return jax.nn.softmax(x, axis=axis)

def _gelu(x):
    return jax.nn.gelu(x, approximate=True)

def _silu(x):
    return jax.nn.silu(x)

def _sigmoid(x):
    return jax.nn.sigmoid(x)

def _layernorm(x, axis=-1, eps=1e-05):
    m = jnp.mean(x, axis=axis, keepdims=True)
    v = jnp.var(x, axis=axis, keepdims=True)
    return (x - m) / jnp.sqrt(v + eps)

def _scatter_add(tgt, idx, src, axis=0):
    return tgt.at[idx].add(src)

def _segment_sum(src, seg, n):
    return jax.ops.segment_sum(src, seg, n)
kernel_name = 'mk_gnn_resnorm_d2_gnn_r32_2594b8'

def setup_inputs(seed: int=0):
    np.random.seed(seed)
    _w = jnp.asarray

    def _rec_inputs():
        import jax
        import jax.numpy as jnp
        _gk = jax.random.key(seed)
        x = -0.0009044 + 1 * jax.random.normal(jax.random.fold_in(_gk, 1), (3125, 16), jnp.float32)
        _s = jax.random.randint(jax.random.fold_in(_gk, 2), (50000,), 0, 3125, jnp.int32)
        _d = jax.random.randint(jax.random.fold_in(_gk, 3), (50000,), 0, 3125, jnp.int32)
        _loop = jnp.arange(3125, dtype=jnp.int32)
        src = jnp.concatenate([_s, _d, _loop])
        dst = jnp.concatenate([_d, _s, _loop])
        _o = jnp.argsort(dst, stable=True)
        src = src[_o]
        dst = dst[_o]
        edge_attr_13 = 2.91757e-06 + 0.999892 * jax.random.normal(jax.random.fold_in(_gk, 12), (103125, 13), jnp.float32)
        return (x, src, dst, edge_attr_13)
    x, src, dst, edge_attr_13 = _rec_inputs()

    def _L0_gnn_setup():
        import jax, jax.numpy as jnp
        import numpy as np
        N_NODES = 3125
        N_EDGES = 100000
        FEAT = 16

        def gcn_conv(x, src, dst, W, b):
            n = x.shape[0]
            loop = jnp.arange(n, dtype=src.dtype)
            s = jnp.concatenate([src, loop])
            d = jnp.concatenate([dst, loop])
            deg = jax.ops.segment_sum(jnp.ones_like(d, dtype=x.dtype), d, num_segments=n)
            dinv = jnp.where(deg > 0, jax.lax.rsqrt(deg), 0.0)
            norm = dinv[s] * dinv[d]
            h = x @ W
            msg = h[s] * norm[:, None]
            out = jax.ops.segment_sum(msg, d, num_segments=n)
            return out + b
        key = jax.random.key(seed)
        k1, k2, k3, k4 = jax.random.split(key, 4)
        scale = 1.0 / np.sqrt(FEAT)
        return {'x': jax.random.normal(k1, (N_NODES, FEAT), dtype=jnp.float32), 'edge_index': jax.random.randint(k2, (2, N_EDGES), 0, N_NODES, dtype=jnp.int64) if jax.config.jax_enable_x64 else jax.random.randint(k2, (2, N_EDGES), 0, N_NODES, dtype=jnp.int32), 'W1': jax.random.normal(k3, (FEAT, 16), dtype=jnp.float32) * scale, 'b1': jnp.zeros((16,), dtype=jnp.float32), 'W2': jax.random.normal(k4, (16, FEAT), dtype=jnp.float32) * scale, 'b2': jnp.zeros((FEAT,), dtype=jnp.float32)}
    _L0_gnn_all = _L0_gnn_setup()
    _L0_gnn_in = {k: v for k, v in _L0_gnn_all.items() if k in ('W1', 'b1', 'W2', 'b2')}
    del _L0_gnn_all

    def _L1_gnn_setup():
        import jax, jax.numpy as jnp
        import numpy as np
        N = 50000
        E = 25000
        NC = 16
        FDIM = 13
        HID = 32
        NREPEATS = 2

        def _gru_cell(x, h, w_ih, w_hh, b_ih, b_hh):
            gi = x @ w_ih.T + b_ih
            gh = h @ w_hh.T + b_hh
            i_r, i_z, i_n = jnp.split(gi, 3, axis=1)
            h_r, h_z, h_n = jnp.split(gh, 3, axis=1)
            r = jax.nn.sigmoid(i_r + h_r)
            z = jax.nn.sigmoid(i_z + h_z)
            n = jnp.tanh(i_n + r * h_n)
            return (1.0 - z) * n + z * h
        key = jax.random.key(seed)
        ks = jax.random.split(key, 10)
        hx = jax.random.normal(ks[0], (N, NC), dtype=jnp.float32)
        edgefeats = jax.random.normal(ks[1], (E, FDIM), dtype=jnp.float32)
        edge_src = jax.random.randint(ks[2], (E,), 0, N, dtype=jnp.int32)
        edge_dst = jax.random.randint(ks[3], (E,), 0, N, dtype=jnp.int32)
        fnet_w1 = jax.random.normal(ks[4], (FDIM, HID), dtype=jnp.float32) * (1.0 / np.sqrt(FDIM))
        fnet_b1 = jnp.zeros((HID,), dtype=jnp.float32)
        fnet_w2 = jax.random.normal(ks[5], (HID, NC * NC), dtype=jnp.float32) * (0.1 / np.sqrt(HID))
        fnet_b2 = jnp.zeros((NC * NC,), dtype=jnp.float32)
        gru_w_ih = jax.random.normal(ks[6], (3 * NC, NC), dtype=jnp.float32) * (1.0 / np.sqrt(NC))
        gru_w_hh = jax.random.normal(ks[7], (3 * NC, NC), dtype=jnp.float32) * (1.0 / np.sqrt(NC))
        gru_b_ih = jnp.zeros((3 * NC,), dtype=jnp.float32)
        gru_b_hh = jnp.zeros((3 * NC,), dtype=jnp.float32)
        return {'hx': hx, 'edgefeats': edgefeats, 'edge_src': edge_src, 'edge_dst': edge_dst, 'fnet_w1': fnet_w1, 'fnet_b1': fnet_b1, 'fnet_w2': fnet_w2, 'fnet_b2': fnet_b2, 'gru_w_ih': gru_w_ih, 'gru_w_hh': gru_w_hh, 'gru_b_ih': gru_b_ih, 'gru_b_hh': gru_b_hh}
    _L1_gnn_all = _L1_gnn_setup()
    _L1_gnn_in = {k: v for k, v in _L1_gnn_all.items() if k in ('fnet_w1', 'fnet_b1', 'fnet_w2', 'fnet_b2', 'gru_w_ih', 'gru_w_hh', 'gru_b_ih', 'gru_b_hh')}
    del _L1_gnn_all
    return {'x': x, 'src': src, 'dst': dst, 'edge_attr_13': edge_attr_13, 'L0_gnn_W1': _L0_gnn_in['W1'], 'L0_gnn_b1': _L0_gnn_in['b1'], 'L0_gnn_W2': _L0_gnn_in['W2'], 'L0_gnn_b2': _L0_gnn_in['b2'], 'L1_gnn_fnet_w1': _L1_gnn_in['fnet_w1'], 'L1_gnn_fnet_b1': _L1_gnn_in['fnet_b1'], 'L1_gnn_fnet_w2': _L1_gnn_in['fnet_w2'], 'L1_gnn_fnet_b2': _L1_gnn_in['fnet_b2'], 'L1_gnn_gru_w_ih': _L1_gnn_in['gru_w_ih'], 'L1_gnn_gru_w_hh': _L1_gnn_in['gru_w_hh'], 'L1_gnn_gru_b_ih': _L1_gnn_in['gru_b_ih'], 'L1_gnn_gru_b_hh': _L1_gnn_in['gru_b_hh']}

def reference(x, src, dst, edge_attr_13, L0_gnn_W1, L0_gnn_b1, L0_gnn_W2, L0_gnn_b2, L1_gnn_fnet_w1, L1_gnn_fnet_b1, L1_gnn_fnet_w2, L1_gnn_fnet_b2, L1_gnn_gru_w_ih, L1_gnn_gru_w_hh, L1_gnn_gru_b_ih, L1_gnn_gru_b_hh):
    import jax
    import jax.numpy as jnp

    def _L0_gnn_ref(x, edge_index, W1, b1, W2, b2):
        import jax, jax.numpy as jnp
        import numpy as np
        N_NODES = 3125
        N_EDGES = 100000
        FEAT = 16

        def gcn_conv(x, src, dst, W, b):
            n = x.shape[0]
            loop = jnp.arange(n, dtype=src.dtype)
            s = jnp.concatenate([src, loop])
            d = jnp.concatenate([dst, loop])
            deg = jax.ops.segment_sum(jnp.ones_like(d, dtype=x.dtype), d, num_segments=n)
            dinv = jnp.where(deg > 0, jax.lax.rsqrt(deg), 0.0)
            norm = dinv[s] * dinv[d]
            h = x @ W
            msg = h[s] * norm[:, None]
            out = jax.ops.segment_sum(msg, d, num_segments=n)
            return out + b
        src, dst = (edge_index[0], edge_index[1])
        h = gcn_conv(x, src, dst, W1, b1)
        h = jax.nn.relu(h)
        out = gcn_conv(h, src, dst, W2, b2)
        return out

    def _L1_gnn_ref(hx, edgefeats, edge_src, edge_dst, fnet_w1, fnet_b1, fnet_w2, fnet_b2, gru_w_ih, gru_w_hh, gru_b_ih, gru_b_hh):
        import jax, jax.numpy as jnp
        import numpy as np
        N = 50000
        E = 25000
        NC = 16
        FDIM = 13
        HID = 32
        NREPEATS = 2

        def _gru_cell(x, h, w_ih, w_hh, b_ih, b_hh):
            gi = x @ w_ih.T + b_ih
            gh = h @ w_hh.T + b_hh
            i_r, i_z, i_n = jnp.split(gi, 3, axis=1)
            h_r, h_z, h_n = jnp.split(gh, 3, axis=1)
            r = jax.nn.sigmoid(i_r + h_r)
            z = jax.nn.sigmoid(i_z + h_z)
            n = jnp.tanh(i_n + r * h_n)
            return (1.0 - z) * n + z * h
        n_nodes, nc = hx.shape
        w = jax.nn.relu(edgefeats @ fnet_w1 + fnet_b1) @ fnet_w2 + fnet_b2
        W = w.reshape(-1, nc, nc)
        deg = jax.ops.segment_sum(jnp.ones((edge_dst.shape[0],), hx.dtype), edge_dst, num_segments=n_nodes)
        inv_deg = 1.0 / jnp.maximum(deg, 1.0)
        for _ in range(NREPEATS):
            xj = hx[edge_src]
            m = jnp.einsum('ei,eio->eo', xj, W)
            agg = jax.ops.segment_sum(m, edge_dst, num_segments=n_nodes)
            agg = agg * inv_deg[:, None]
            hx = _gru_cell(agg, hx, gru_w_ih, gru_w_hh, gru_b_ih, gru_b_hh)
        return hx
    edge_index = jnp.stack([src, dst])
    x = _layernorm(x + _L0_gnn_ref(x, edge_index, L0_gnn_W1, L0_gnn_b1, L0_gnn_W2, L0_gnn_b2), axis=-1)
    x = _layernorm(x + _L1_gnn_ref(x, edge_attr_13, src, dst, L1_gnn_fnet_w1, L1_gnn_fnet_b1, L1_gnn_fnet_w2, L1_gnn_fnet_b2, L1_gnn_gru_w_ih, L1_gnn_gru_w_hh, L1_gnn_gru_b_ih, L1_gnn_gru_b_hh), axis=-1)
    return x

_drawn_inputs = setup_inputs


def setup_inputs(seed=0):
    import zlib

    import numpy as np

    out = dict(_drawn_inputs(seed))
    spreads = {'L0_gnn_b1': (0.0, 0.1),
     'L0_gnn_b2': (0.0, 0.1),
     'L1_gnn_fnet_b1': (0.0, 0.8),
     'L1_gnn_fnet_b2': (0.0, 0.275),
     'L1_gnn_gru_b_ih': (0.0, 0.1),
     'L1_gnn_gru_b_hh': (0.0, 0.287)}
    factors = {'edge_attr_13': 3.961, 'L1_gnn_fnet_w1': 3.917, 'L1_gnn_fnet_w2': 2.815}
    for name, (base, spread) in spreads.items():
        noise = np.random.default_rng([zlib.crc32(name.encode()), seed]).standard_normal(out[name].shape)
        drawn = base * np.exp(spread * noise) if base else spread * noise
        out[name] = jnp.asarray(drawn.astype(out[name].dtype))
    for name, factor in factors.items():
        out[name] = (out[name] * factor).astype(out[name].dtype)
    return out
```

```python
import concourse.bass as bass
from concourse import mybir
from contextlib import ExitStack

NODES, FEAT, EDGES, EDGE_FEAT, HIDDEN = 3125, 16, 103125, 13, 32
P = 125
NT = NODES // P
TILES = EDGES // P
CH = 11
CHUNKS = TILES // CH
WIN = 8
SLOTS = CH * WIN
SPAN = 64
BLK = 456
BLOCKS = 7
ACCW = BLK * BLOCKS
GATES = 3 * FEAT
CW = CH * HIDDEN
XW = CH * WIN * FEAT
PAIRS = 34
DEG, GCN1, GCN2, GRU1, GRU2 = range(5)


def gnn_kernel(nc, x_in, src_in, dst_in, first_in, edge_t, w1_in, b1_in, gw1_in, gb1_in, gw2_in, gb2_in,
               w2_in, b2_in, wih_t, whh_t, bih_in, bhh_in, ident_in, iota_in, slot_in, out):
    f32, i32 = mybir.dt.float32, mybir.dt.int32
    ALU, ACT, AX = mybir.AluOpType, mybir.ActivationFunctionType, mybir.AxisListType
    ds = bass.ds
    ctx = ExitStack()
    with ctx:
        def sb(name, shape, dt=f32):
            return ctx.enter_context(nc.sbuf_tensor(name, shape, dt))

        def sem(name):
            return ctx.enter_context(nc.semaphore(name))

        src_i = sb("src_i", [P, TILES], i32)
        dst_i = sb("dst_i", [P, TILES], i32)
        dst_f = sb("dst_f", [P, TILES])
        onehot = sb("onehot", [P, TILES, WIN])
        hidden = sb("hidden", [P, TILES * HIDDEN])
        slot_node = sb("slot_node", [SLOTS, CHUNKS])
        first_i = sb("first_i", [CH, CHUNKS], i32)
        first_f = sb("first_f", [CH + 1, CHUNKS])
        ident = sb("ident", [P, P])
        iota = sb("iota", [P, BLK])
        slot_matrix = sb("slot_matrix", [CH + 1, SLOTS])
        ones = sb("ones", [P, P])
        w1b1 = sb("w1b1", [EDGE_FEAT + 1, HIDDEN])
        w2q = sb("w2q", [128, 4, FEAT])
        b2m = sb("b2m", [FEAT, FEAT])
        w2row = sb("w2row", [HIDDEN, FEAT * FEAT])
        b2row = sb("b2row", [1, FEAT * FEAT])
        gw = [sb("gw1", [FEAT, FEAT]), sb("gw2", [FEAT, FEAT])]
        gb = [sb("gb1", [P, FEAT]), sb("gb2", [P, FEAT])]
        wih = sb("wih", [FEAT, GATES])
        whh = sb("whh", [FEAT, GATES])
        bih = sb("bih", [P, GATES])
        bhh = sb("bhh", [P, GATES])
        idx = [sb(f"idx{s}", [P, CH], i32) for s in range(2)]
        xsrc = [sb(f"xsrc{s}", [P, CH, FEAT]) for s in range(2)]
        hidden_ring = [sb(f"hidden_ring{s}", [P, CW]) for s in range(2)]
        sums_sb = [sb(f"sums_sb{s}", [128, CW]) for s in range(2)]
        xsum_sb = [sb(f"xsum_sb{s}", [FEAT, SLOTS]) for s in range(2)]
        slots_sb = [sb(f"slots_sb{s}", [SLOTS, FEAT]) for s in range(2)]
        place = [sb(f"place{s}", [SLOTS, SPAN]) for s in range(2)]
        scratch = sb("scratch", [P, 3 * NT * GATES])
        edges_sb = [scratch[0:EDGE_FEAT + 1, s * CH * P:(s + 1) * CH * P] for s in range(2)]
        xwin = [scratch[:, s * XW:(s + 1) * XW] for s in range(2)]
        wide = scratch[:, 0:ACCW]
        gate_i, gate_h, gate_n = (scratch[:, k * NT * GATES:(k + 1) * NT * GATES]
                                  .rearrange("p (t g) -> p t g", g=GATES) for k in range(3))
        acc = sb("acc", [FEAT, ACCW])
        table_t = sb("table_t", [FEAT, NODES])
        x0 = sb("x0", [P, NT, FEAT])
        x1 = sb("x1", [P, NT, FEAT])
        table = sb("table", [P, NT, FEAT])
        y = sb("y", [P, NT, FEAT])
        z = sb("z", [P, NT, FEAT])
        dinv = sb("dinv", [P, NT, 1])
        inv_deg = sb("inv_deg", [P, NT, 1])
        stat = sb("stat", [P, NT, 1])
        var = sb("var", [P, NT, 1])
        worst = sb("worst", [P, 4])
        flag_f = sb("flag_f", [1, 1])
        flag_i = sb("flag_i", [1, 1], i32)
        g_idx = sb("g_idx", [P, 1], i32)
        g_x = sb("g_x", [P, FEAT])
        g_hidden = sb("g_hidden", [P, HIDDEN])
        g_hidden_t = sb("g_hidden_t", [HIDDEN, P])
        g_prod = sb("g_prod", [P, FEAT, FEAT])
        g_msg = sb("g_msg", [P, FEAT])

        bank = [ctx.enter_context(nc.psum_tensor(f"bank{i}", [128, 512], f32)) for i in range(8)]
        sum_bank, slot_bank, place_bank, mlp_bank = bank[0:2], bank[2:4], bank[4:6], bank[6:8]

        tables = [None] + [nc.dram_tensor(f"table_dram{k}", [NODES, FEAT], f32).ap() for k in range(1, 5)]

        ints_in = sem("ints_in")
        consts_in = sem("consts_in")
        edges_in = [sem(f"edges_in{s}") for s in range(2)]
        dst_ready = sem("dst_ready")
        bases_ready = sem("bases_ready")
        flags_sum = sem("flags_sum")
        flag_ready = sem("flag_ready")
        v_step = sem("v_step")
        onehot_ready = sem("onehot_ready")
        acc_zero = sem("acc_zero")
        idx_ready = sem("idx_ready")
        gather_turn = sem("gather_turn")
        gathered = [None] + [[sem(f"gathered{k}_{s}") for s in range(2)] for k in range(1, 5)]
        xwin_ready = sem("xwin_ready")
        place_ready = sem("place_ready")
        summed = sem("summed")
        xsum_copied = sem("xsum_copied")
        slotted = sem("slotted")
        slots_copied = sem("slots_copied")
        placed = sem("placed")
        added = sem("added")
        mlp_done = sem("mlp_done")
        hidden_ready = sem("hidden_ready")
        hidden_copied = sem("hidden_copied")
        g_idx_ready = sem("g_idx_ready")
        g_gathered = [None] + [sem(f"g_gathered{k}") for k in range(1, 5)]
        g_hidden_copied = sem("g_hidden_copied")
        g_transposed = sem("g_transposed")
        g_hidden_ready = sem("g_hidden_ready")
        g_weights = sem("g_weights")
        g_prod_ready = sem("g_prod_ready")
        g_msg_ready = sem("g_msg_ready")
        g_wide_ready = sem("g_wide_ready")
        g_blocks = sem("g_blocks")
        g_added = sem("g_added")
        table_ready = sem("table_ready")
        table_stored = sem("table_stored")
        table_turned = sem("table_turned")
        table_t_ready = sem("table_t_ready")
        node_sums = sem("node_sums")
        node_hidden = sem("node_hidden")
        node_free = sem("node_free")
        rz_in = sem("rz_in")
        rz_out = sem("rz_out")
        n_in = sem("n_in")
        n_out = sem("n_out")
        sqrt_in = sem("sqrt_in")
        sqrt_out = sem("sqrt_out")
        out_ready = sem("out_ready")
        out_stored = sem("out_stored")

        N_CONSTS = 20
        ROOTS = (DEG, GCN2, GRU2)

        def steps(eng, step):
            for c in range(5):
                step(c, c % 2)
            with eng.Fori(0, PAIRS) as i:
                step(i * 2 + 5, 1)
                step(i * 2 + 6, 0)
            for c in (73, 74):
                step(c, c % 2)

        def acc_view(t):
            return acc[:, 0:NODES].rearrange("f (p t) -> f t p", t=NT)[:, t, :]

        block = ctx.enter_context(nc.Block())

        @block.sync
        def _(sp):
            sp.dma_start(dst_i[:, :], dst_in).then_inc(ints_in, 16)
            sp.dma_start(first_i[:, :], first_in).then_inc(ints_in, 16)
            sp.dma_start(src_i[:, :], src_in).then_inc(ints_in, 16)
            loads = [(ident[:, :], ident_in), (iota[:, :], iota_in), (slot_matrix[:, :], slot_in),
                     (x0[:, :, :], x_in.rearrange("(p t) f -> p t f", t=NT)),
                     (w1b1[0:EDGE_FEAT, :], w1_in), (w1b1[EDGE_FEAT:EDGE_FEAT + 1, :], b1_in),
                     (b2m[:, :], b2_in.rearrange("a (i o) -> (a i) o", o=FEAT)), (b2row[:, :], b2_in),
                     (w2row[:, :], w2_in), (gw[0][:, :], gw1_in), (gw[1][:, :], gw2_in),
                     (wih[:, :], wih_t), (whh[:, :], whh_t)]
            loads += [(w2q[q * HIDDEN:(q + 1) * HIDDEN, :, :],
                       w2_in[:, q * 64:(q + 1) * 64].rearrange("k (i o) -> k i o", o=FEAT)) for q in range(4)]
            loads += [(gb[0][:, :], gb1_in.to_broadcast([P, FEAT])), (gb[1][:, :], gb2_in.to_broadcast([P, FEAT])),
                      (bih[:, :], bih_in.to_broadcast([P, GATES])), (bhh[:, :], bhh_in.to_broadcast([P, GATES]))]
            assert len(loads) == N_CONSTS + 1
            for to, what in loads:
                sp.dma_start(to, what).then_inc(consts_in, 16)

            def load_edges(c, s):
                if not isinstance(c, int) or c >= 2:
                    sp.wait_ge(mlp_done, c - 1)
                sp.dma_start(edges_sb[s][0:EDGE_FEAT, :], edge_t[:, ds(c * (CH * P), CH * P)]).then_inc(edges_in[s], 16)

            for k in range(1, 5):
                sp.wait_ge(table_ready, k)
                sp.dma_start(tables[k].rearrange("(p t) f -> p t f", t=NT), table[:, :, :]).then_inc(table_stored, 16)
                if k == GCN1:
                    steps(sp, load_edges)
            sp.wait_ge(table_stored, 64)
            sp.wait_ge(out_ready, 1)
            sp.dma_start(out.rearrange("(p t) f -> p t f", t=NT), y[:, :, :]).then_inc(out_stored, 16)
            sp.wait_ge(out_stored, 16)

        @block.gpsimd
        def _(pool):
            pool.wait_ge(flag_ready, 1)
            general = pool.value_load(flag_i[0:1, 0:1], min_val=0, max_val=1)
            for ph in range(GCN1, GRU2 + 1):
                pool.wait_ge(table_stored, 16 * ph)
                with pool.If(general < 1):
                    def gather(c, s):
                        pool.wait_ge(idx_ready, c + (1 + (ph - 1) * CHUNKS))
                        if not isinstance(c, int) or c >= 2:
                            pool.wait_ge(summed, c + (ph * CHUNKS - 1))
                        pool.sem_inc(gather_turn, 1)
                        for j in range(CH):
                            pool.indirect_dma_start(
                                out=xsrc[s][:, j, :], out_offset=None, in_=tables[ph],
                                in_offset=bass.IndirectOffsetOnAxis(ap=idx[s][:, j:j + 1], axis=0)
                            ).then_inc(gathered[ph][s], 16)
                    steps(pool, gather)
                with pool.Else():
                    with pool.Fori(0, TILES) as t:
                        pool.wait_ge(g_idx_ready, t + (1 + (ph - 1) * TILES))
                        pool.sem_inc(gather_turn, 1)
                        pool.indirect_dma_start(
                            out=g_x[:, :], out_offset=None, in_=tables[ph],
                            in_offset=bass.IndirectOffsetOnAxis(ap=g_idx[:, 0:1], axis=0)
                        ).then_inc(g_gathered[ph], 16)
                pool.nop()

        @block.scalar
        def _(act):
            act.wait_ge(flag_ready, 1)
            general = act.value_load(flag_i[0:1, 0:1], min_val=0, max_val=1)

            def relu_hidden(c, s):
                act.wait_ge(mlp_done, c + 1)
                nc.scalar.activation(hidden[:, ds(c * CW, CW)], mlp_bank[s][0:P, 0:CW], ACT.Relu).then_inc(hidden_ready, 1)

            def copy_hidden(ph, c, s):
                if not isinstance(c, int) or c >= 2:
                    act.wait_ge(summed, c + (ph * CHUNKS - 1))
                nc.scalar.activation(hidden_ring[s][:, :], hidden[:, ds(c * CW, CW)], ACT.Copy).then_inc(hidden_copied, 1)

            def copy_sums(ph, c, s):
                act.wait_ge(summed, c + (1 + ph * CHUNKS))
                if not isinstance(c, int) or c >= 2:
                    act.wait_ge(slotted, c + (ph * CHUNKS - 1))
                if ph >= GRU1:
                    nc.scalar.activation(sums_sb[s][:, :], sum_bank[s][:, 0:CW], ACT.Copy)
                nc.scalar.activation(xsum_sb[s][:, :], sum_bank[s][0:FEAT, CW:CW + SLOTS], ACT.Copy).then_inc(xsum_copied, 1)

            def copy_slots(ph, c, s):
                act.wait_ge(slotted, c + (1 + ph * CHUNKS))
                if not isinstance(c, int) or c >= 2:
                    act.wait_ge(placed, c + (ph * CHUNKS - 1))
                nc.scalar.activation(slots_sb[s][:, :], slot_bank[s][0:SLOTS, 0:FEAT], ACT.Copy).then_inc(slots_copied, 1)

            for ph in range(DEG, GRU2 + 1):
                if ph == GRU1:
                    act.wait_ge(hidden_ready, CHUNKS)
                if ph > DEG:
                    act.wait_ge(table_turned, ph)
                    for b in range(7):
                        w = min(4, NT - 4 * b) * P
                        last = nc.scalar.activation(table_t[:, 4 * b * P:4 * b * P + w], bank[b][0:FEAT, 0:w], ACT.Copy)
                    last.then_inc(table_t_ready, 1)
                with act.If(general < 1):
                    def step(c, s):
                        if ph == GCN1:
                            relu_hidden(c, s)
                        if ph >= GRU1:
                            copy_hidden(ph, c, s)
                        copy_sums(ph, c, s)
                        if not isinstance(c, int) or c >= 1:
                            copy_slots(ph, c - 1, 1 - s)
                    steps(act, step)
                    copy_slots(ph, CHUNKS - 1, 0)
                with act.Else():
                    if ph == GCN1:
                        steps(act, relu_hidden)
                    if ph >= GRU1:
                        with act.Fori(0, TILES) as t:
                            act.wait_ge(g_transposed, t + (2 + (ph - GRU1) * TILES))
                            nc.scalar.activation(g_hidden_t[:, :], bank[7][0:HIDDEN, 256:256 + P], ACT.Copy).then_inc(g_hidden_ready, 1)
                act.nop()
                if ph >= GRU1:
                    act.wait_ge(rz_in, ph - GRU1 + 1)
                    nc.scalar.activation(gate_i[:, :, 0:32], gate_i[:, :, 0:32], ACT.Sigmoid).then_inc(rz_out, 1)
                    act.wait_ge(n_in, ph - GRU1 + 1)
                    nc.scalar.activation(gate_n[:, :, 0:16], gate_n[:, :, 0:16], ACT.Tanh).then_inc(n_out, 1)
                if ph in ROOTS:
                    act.wait_ge(sqrt_in, ROOTS.index(ph) + 1)
                    nc.scalar.activation(var[:, :, :], var[:, :, :], ACT.Sqrt).then_inc(sqrt_out, 1)

        @block.vector
        def _(dve):
            chained = [0]

            def link(ins):
                chained[0] += 1
                ins.then_inc(v_step, 1)
                dve.wait_ge(v_step, chained[0])

            for free in (g_blocks, g_added, g_transposed, g_prod_ready):
                dve.sem_inc(free, 1)
            nc.vector.memset(ones[:, :], 1.0)
            link(nc.vector.memset(first_f[:, :], 1.0))
            dve.wait_ge(ints_in, 48)
            nc.vector.tensor_copy(first_f[0:CH, :], first_i[:, :])
            nc.vector.tensor_copy(dst_f[:, :], dst_i[:, :]).then_inc(dst_ready, 1)
            dve.wait_ge(dst_ready, 1)
            dve.wait_ge(consts_in, 16 * (N_CONSTS + 1))
            dve.wait_ge(bases_ready, 1)
            half = 35 * CH
            rel = hidden[:, 0:TILES]
            from_chunk = hidden[:, TILES:2 * TILES]
            for n0, n1, b in ((0, half, 0), (half, TILES, 1)):
                base = bank[b][0:P, 0:n1 - n0]
                nc.vector.tensor_tensor(rel[:, n0:n1], dst_f[:, n0:n1], base, ALU.subtract)
                chunk_base = base.rearrange("p (c j) -> p c j", j=CH)[:, :, 0:1].to_broadcast([P, (n1 - n0) // CH, CH])
                last = nc.vector.tensor_tensor(from_chunk[:, n0:n1].rearrange("p (c j) -> p c j", j=CH),
                                               dst_f[:, n0:n1].rearrange("p (c j) -> p c j", j=CH), chunk_base, ALU.subtract)
            link(last)
            nc.vector.tensor_copy(slot_node[:, :], bank[2][0:SLOTS, 0:CHUNKS])
            nc.vector.tensor_tensor(onehot[:, :, :], rel.rearrange("p (t o) -> p t o", o=1).to_broadcast([P, TILES, WIN]),
                                    iota[:, 0:WIN].rearrange("p (o w) -> p o w", o=1).to_broadcast([P, TILES, WIN]),
                                    ALU.is_equal).then_inc(onehot_ready, 1)
            nc.vector.tensor_reduce(worst[:, 0:1], rel, AX.X, ALU.max)
            nc.vector.tensor_reduce(worst[:, 1:2], from_chunk, AX.X, ALU.max)
            nc.vector.tensor_reduce(worst[:, 2:3], rel, AX.X, ALU.min)
            link(nc.vector.tensor_reduce(worst[:, 3:4], from_chunk, AX.X, ALU.min))
            nc.vector.tensor_scalar(worst[:, 0:1], worst[:, 0:1], float(WIN), None, ALU.is_ge)
            nc.vector.tensor_scalar(worst[:, 1:2], worst[:, 1:2], float(SPAN), None, ALU.is_ge)
            link(nc.vector.tensor_scalar(worst[:, 2:4], worst[:, 2:4], 0.0, None, ALU.is_lt))
            link(nc.vector.tensor_reduce(var[:, 0, :], worst[:, :], AX.X, ALU.max))
            nc.vector.tensor_copy(stat[:, 0, :], var[:, 0, :]).then_inc(flags_sum, 1)
            dve.wait_ge(flags_sum, 2)
            link(nc.vector.tensor_scalar(flag_f[:, :], bank[3][0:1, 0:1], 0.5, None, ALU.is_ge))
            link(nc.vector.tensor_copy(flag_i[:, :], flag_f[:, :]))
            dve.nop().then_inc(flag_ready, 1)
            general = dve.value_load(flag_i[0:1, 0:1], min_val=0, max_val=1)

            def add_placed(ph, c, s):
                first = dve.value_load(dst_i[0:1, ds(c * CH, 1) if not isinstance(c, int) else slice(c * CH, c * CH + 1)],
                                       min_val=0, max_val=NODES - 1)
                dve.wait_ge(placed, c + (1 + ph * CHUNKS))
                if not isinstance(c, int) or c >= 1:
                    dve.wait_ge(added, c + ph * CHUNKS)
                window = acc[:, ds(first, SPAN)]
                nc.vector.tensor_tensor(window, window, place_bank[s][0:FEAT, 0:SPAN], ALU.add).then_inc(added, 1)

            def make_place(ph, c, s):
                if not isinstance(c, int) or c >= 2:
                    dve.wait_ge(placed, c + (ph * CHUNKS - 1))
                nc.vector.tensor_scalar(place[s][:, :], iota[0:SLOTS, 0:SPAN], slot_node[:, ds(c, 1)], None,
                                        ALU.is_equal).then_inc(place_ready, 1)

            def widen(ph, c, s, users):
                dve.wait_ge(gathered[ph][s], users * (16 * CH))
                if ph >= GRU1:
                    if not isinstance(c, int) or c >= 2:
                        dve.wait_ge(summed, c + (ph * CHUNKS - 1))
                    nc.vector.tensor_tensor(
                        xwin[s].rearrange("p (j n i) -> p j n i", n=WIN, i=FEAT),
                        xsrc[s][:, :, :].rearrange("p j (o i) -> p j o i", o=1).to_broadcast([P, CH, WIN, FEAT]),
                        onehot[:, ds(c * CH, CH), :].rearrange("p j (n o) -> p j n o", o=1).to_broadcast([P, CH, WIN, FEAT]),
                        ALU.mult).then_inc(xwin_ready, 1)

            def normalise(to, turn):
                link(nc.vector.tensor_reduce(stat[:, :, :], y[:, :, :], AX.X, ALU.add))
                link(nc.vector.tensor_scalar(stat[:, :, :], stat[:, :, :], 1.0 / FEAT, None, ALU.mult))
                link(nc.vector.tensor_tensor(y[:, :, :], y[:, :, :], stat[:, :, :].to_broadcast([P, NT, FEAT]), ALU.subtract))
                link(nc.vector.tensor_tensor(z[:, :, :], y[:, :, :], y[:, :, :], ALU.mult))
                link(nc.vector.tensor_reduce(var[:, :, :], z[:, :, :], AX.X, ALU.add))
                nc.vector.tensor_scalar(var[:, :, :], var[:, :, :], 1.0 / FEAT, 1e-5, ALU.mult, ALU.add).then_inc(sqrt_in, 1)
                dve.wait_ge(sqrt_out, turn)
                link(nc.vector.reciprocal(var[:, :, :], var[:, :, :]))
                return nc.vector.tensor_tensor(to, y[:, :, :], var[:, :, :].to_broadcast([P, NT, FEAT]), ALU.mult)

            for ph in range(DEG, GRU2 + 1):
                link(nc.vector.memset(acc[:, :], 0.0))
                with dve.If(general < 1):
                    def step(c, s, users):
                        if ph > DEG:
                            if c is not None and not (isinstance(c, int) and c == CHUNKS - 1):
                                other = users - 1 if s == 0 else users
                                if not isinstance(c, int) or c >= 1:
                                    dve.wait_ge(gathered[ph][1 - s], other * (16 * CH))
                                nc.vector.tensor_copy(idx[1 - s][:, :], src_i[:, ds(c * CH + CH, CH)]).then_inc(idx_ready, 1)
                            widen(ph, c, s, users)
                        make_place(ph, c, s)
                        if not isinstance(c, int) or c >= 2:
                            add_placed(ph, c - 2, s)
                    if ph > DEG:
                        nc.vector.tensor_copy(idx[0][:, :], src_i[:, 0:CH]).then_inc(idx_ready, 1)
                    for c in range(5):
                        step(c, c % 2, c // 2 + 1)
                    with dve.Fori(0, PAIRS) as i:
                        step(i * 2 + 5, 1, i + 3)
                        step(i * 2 + 6, 0, i + 4)
                    for c in (73, 74):
                        step(c, c % 2, c // 2 + 1)
                    add_placed(ph, 73, 1)
                    add_placed(ph, 74, 0)
                    dve.wait_ge(added, (ph + 1) * CHUNKS)
                with dve.Else():
                    if ph == GCN1:
                        dve.wait_ge(mlp_done, CHUNKS)
                    with dve.Fori(0, TILES) as t:
                        if ph > DEG:
                            dve.wait_ge(g_blocks, t + (1 + ph * TILES))
                            nc.vector.tensor_copy(g_idx[:, :], src_i[:, ds(t, 1)]).then_inc(g_idx_ready, 1)
                        if ph >= GRU1:
                            dve.wait_ge(g_transposed, t + (1 + (ph - GRU1) * TILES))
                            nc.vector.tensor_copy(g_hidden[:, :], hidden[:, ds(t * HIDDEN, HIDDEN)]).then_inc(g_hidden_copied, 1)
                        dve.wait_ge(g_blocks, t + (1 + ph * TILES))
                        for b in range(BLOCKS):
                            last = nc.vector.tensor_scalar(wide[:, b * BLK:(b + 1) * BLK], iota[:, :], float(b * BLK),
                                                           dst_f[:, ds(t, 1)], ALU.add, ALU.is_equal)
                        last.then_inc(g_wide_ready, 1)
                        if ph > DEG:
                            dve.wait_ge(g_gathered[ph], t * 16 + 16)
                        if ph >= GRU1:
                            dve.wait_ge(g_weights, t + (1 + (ph - GRU1) * TILES))
                            nc.vector.tensor_tensor(g_prod[:, :, :], bank[7][0:P, 0:FEAT * FEAT].rearrange("p (i o) -> p i o", o=FEAT),
                                                    g_x[:, :].rearrange("p (i o) -> p i o", o=1).to_broadcast([P, FEAT, FEAT]),
                                                    ALU.mult).then_inc(g_prod_ready, 1)
                            dve.wait_ge(g_prod_ready, t + (2 + (ph - GRU1) * TILES))
                            nc.vector.tensor_reduce(g_msg[:, :], g_prod[:, :, :].rearrange("p i o -> p o i"), AX.X, ALU.add).then_inc(g_msg_ready, 1)
                        dve.wait_ge(g_blocks, t + (2 + ph * TILES))
                        dve.wait_ge(g_added, t + (1 + ph * TILES))
                        for b in range(BLOCKS):
                            part = acc[:, b * BLK:(b + 1) * BLK]
                            last = nc.vector.tensor_tensor(part, part, bank[b][0:FEAT, 0:BLK], ALU.add)
                        last.then_inc(g_added, 1)
                    dve.wait_ge(g_added, 1 + (ph + 1) * TILES)
                dve.nop().then_inc(node_free, 1)
                dve.wait_ge(node_sums, ph + 1)
                if ph == DEG:
                    count = bank[7][0:P, 0:NT * FEAT].rearrange("p (t f) -> p t f", f=FEAT)[:, :, 0:1]
                    nc.vector.tensor_scalar(stat[:, :, :], count, 1.0, None, ALU.max)
                    nc.vector.tensor_scalar(var[:, :, :], count, 1.0, None, ALU.add).then_inc(sqrt_in, 1)
                    dve.wait_ge(sqrt_out, 1)
                    link(nc.vector.reciprocal(dinv[:, :, :], var[:, :, :]))
                    link(nc.vector.reciprocal(inv_deg[:, :, :], stat[:, :, :]))
                    link(nc.vector.memset(scratch[0:EDGE_FEAT + 1, 0:2 * CH * P], 1.0))
                    nc.vector.tensor_tensor(table[:, :, :], x0[:, :, :], dinv[:, :, :].to_broadcast([P, NT, FEAT]),
                                            ALU.mult).then_inc(table_ready, 1)
                elif ph <= GCN2:
                    conv = bank[7][0:P, 0:NT * FEAT].rearrange("p (t f) -> p t f", f=FEAT)
                    link(nc.vector.tensor_tensor(y[:, :, :], conv, dinv[:, :, :].to_broadcast([P, NT, FEAT]), ALU.mult))
                    link(nc.vector.tensor_tensor(y[:, :, :], y[:, :, :], gb[ph - GCN1][:, :].rearrange("p (o f) -> p o f", o=1)
                                                 .to_broadcast([P, NT, FEAT]), ALU.add))
                    dve.wait_ge(table_stored, 16 * ph)
                    dve.wait_ge(table_turned, ph)
                    if ph == GCN1:
                        link(nc.vector.tensor_scalar(y[:, :, :], y[:, :, :], 0.0, None, ALU.max))
                        nc.vector.tensor_tensor(table[:, :, :], y[:, :, :], dinv[:, :, :].to_broadcast([P, NT, FEAT]),
                                                ALU.mult).then_inc(table_ready, 1)
                    else:
                        link(nc.vector.tensor_tensor(y[:, :, :], y[:, :, :], x0[:, :, :], ALU.add))
                        link(normalise(x1[:, :, :], 2))
                        nc.vector.tensor_copy(table[:, :, :], x1[:, :, :]).then_inc(table_ready, 1)
                else:
                    def wide3(ap, w):
                        return ap.to_broadcast([P, NT, w])

                    def bias(ap, w):
                        return ap.rearrange("p (o g) -> p o g", o=1).to_broadcast([P, NT, w])
                    for b in range(3):
                        t0, t1 = 10 * b, min(10 * b + 10, NT)
                        w = (t1 - t0) * GATES
                        nc.vector.tensor_tensor(gate_i[:, t0:t1, :], bank[b][0:P, 0:w].rearrange("p (t g) -> p t g", g=GATES),
                                                inv_deg[:, t0:t1, :].to_broadcast([P, t1 - t0, GATES]), ALU.mult)
                        last = nc.vector.tensor_tensor(gate_h[:, t0:t1, :], bank[3 + b][0:P, 0:w].rearrange("p (t g) -> p t g", g=GATES),
                                                       bhh[:, :].rearrange("p (o g) -> p o g", o=1).to_broadcast([P, t1 - t0, GATES]), ALU.add)
                    link(last)
                    link(nc.vector.tensor_tensor(gate_i[:, :, :], gate_i[:, :, :], bias(bih[:, :], GATES), ALU.add))
                    nc.vector.tensor_tensor(gate_i[:, :, 0:32], gate_i[:, :, 0:32], gate_h[:, :, 0:32], ALU.add).then_inc(rz_in, 1)
                    dve.wait_ge(rz_out, ph - GRU1 + 1)
                    link(nc.vector.tensor_tensor(gate_n[:, :, 0:16], gate_i[:, :, 0:16], gate_h[:, :, 32:48], ALU.mult))
                    nc.vector.tensor_tensor(gate_n[:, :, 0:16], gate_n[:, :, 0:16], gate_i[:, :, 32:48], ALU.add).then_inc(n_in, 1)
                    dve.wait_ge(n_out, ph - GRU1 + 1)
                    link(nc.vector.tensor_tensor(y[:, :, :], table[:, :, :], gate_n[:, :, 0:16], ALU.subtract))
                    link(nc.vector.tensor_tensor(y[:, :, :], y[:, :, :], gate_i[:, :, 16:32], ALU.mult))
                    link(nc.vector.tensor_tensor(y[:, :, :], y[:, :, :], gate_n[:, :, 0:16], ALU.add))
                    if ph == GRU1:
                        dve.wait_ge(table_stored, 16 * ph)
                        dve.wait_ge(table_turned, ph)
                        nc.vector.tensor_copy(table[:, :, :], y[:, :, :]).then_inc(table_ready, 1)
                    else:
                        link(nc.vector.tensor_tensor(y[:, :, :], y[:, :, :], x1[:, :, :], ALU.add))
                        link(normalise(z[:, :, :], 3))
                        nc.vector.tensor_copy(y[:, :, :], z[:, :, :]).then_inc(out_ready, 1)

        @block.tensor
        def _(pe):
            mm = nc.tensor.matmul
            pe.wait_ge(dst_ready, 1)
            pe.wait_ge(consts_in, 16 * (N_CONSTS + 1))
            half = 35 * CH
            mm(bank[0][0:P, 0:half], ones[0:1, :], dst_f[0:1, 0:half], start=True, stop=True)
            mm(bank[1][0:P, 0:TILES - half], ones[0:1, :], dst_f[0:1, half:TILES], start=True, stop=True)
            mm(bank[2][0:SLOTS, 0:CHUNKS], slot_matrix[:, :], first_f[:, :], start=True, stop=True).then_inc(bases_ready, 1)
            pe.wait_ge(flags_sum, 1)
            mm(bank[3][0:1, 0:1], stat[:, 0, :], ones[:, 0:1], start=True, stop=True).then_inc(flags_sum, 1)
            pe.wait_ge(flag_ready, 1)
            general = pe.value_load(flag_i[0:1, 0:1], min_val=0, max_val=1)
            pe.wait_ge(onehot_ready, 1)

            def edge_mlp(c, s, users):
                pe.wait_ge(edges_in[s], users * 16)
                if not isinstance(c, int) or c >= 2:
                    pe.wait_ge(hidden_ready, c - 1)
                for j in range(CH):
                    last = mm(mlp_bank[s][0:P, j * HIDDEN:(j + 1) * HIDDEN], edges_sb[s][:, j * P:(j + 1) * P],
                              w1b1[:, :], start=True, stop=True)
                last.then_inc(mlp_done, 1)

            def window_sums(ph, c, s, users):
                if not isinstance(c, int) or c >= 2:
                    pe.wait_ge(xsum_copied, c + (ph * CHUNKS - 1))
                if ph == DEG:
                    mm(sum_bank[s][0:FEAT, CW:CW + SLOTS], ones[:, 0:FEAT], onehot[:, ds(c * CH, CH), :],
                       start=True, stop=True).then_inc(summed, 1)
                    return
                pe.wait_ge(gathered[ph][s], users * (16 * CH))
                if ph >= GRU1:
                    pe.wait_ge(xwin_ready, c + (1 + (ph - GRU1) * CHUNKS))
                    pe.wait_ge(hidden_copied, c + (1 + (ph - GRU1) * CHUNKS))
                for j in range(CH):
                    if ph >= GRU1:
                        win = xwin[s][:, j * 128:(j + 1) * 128].rearrange("p (n i) -> p n i", i=FEAT)
                        for q in range(4):
                            mm(sum_bank[s][q * 32:(q + 1) * 32, j * 32:(j + 1) * 32],
                               hidden_ring[s][:, j * HIDDEN:(j + 1) * HIDDEN], win[:, :, q * 4:(q + 1) * 4],
                               start=True, stop=True, tile_position=(0, 32 * q))
                    last = mm(sum_bank[s][0:FEAT, CW + j * WIN:CW + (j + 1) * WIN], xsrc[s][:, j, :],
                              onehot[:, ds(c * CH + j, 1), :], start=True, stop=True)
                last.then_inc(summed, 1)

            def slot_sums(ph, c, s):
                pe.wait_ge(xsum_copied, c + (1 + ph * CHUNKS))
                if not isinstance(c, int) or c >= 2:
                    pe.wait_ge(slots_copied, c + (ph * CHUNKS - 1))
                to = slot_bank[s][0:SLOTS, 0:FEAT]
                if ph >= GRU1:
                    part = sums_sb[s][:, :].rearrange("p (m r) -> p r m", r=4)
                    for r in range(4):
                        mm(to, part[:, r, :], w2q[:, r, :], start=(r == 0), stop=False)
                    mm(to, xsum_sb[s][:, :], b2m[:, :], start=False, stop=True).then_inc(slotted, 1)
                else:
                    mm(to, xsum_sb[s][:, :], ident[0:FEAT, 0:FEAT], start=True, stop=True).then_inc(slotted, 1)

            def place_slots(ph, c, s):
                pe.wait_ge(slots_copied, c + (1 + ph * CHUNKS))
                pe.wait_ge(place_ready, c + (1 + ph * CHUNKS))
                if not isinstance(c, int) or c >= 2:
                    pe.wait_ge(added, c + (ph * CHUNKS - 1))
                mm(place_bank[s][0:FEAT, 0:SPAN], slots_sb[s][:, :], place[s][:, :], start=True, stop=True).then_inc(placed, 1)

            def pe_steps(step):
                for c in range(5):
                    step(c, c % 2, c // 2 + 1)
                with pe.Fori(0, PAIRS) as i:
                    step(i * 2 + 5, 1, i + 3)
                    step(i * 2 + 6, 0, i + 4)
                for c in (73, 74):
                    step(c, c % 2, c // 2 + 1)

            for ph in range(DEG, GRU2 + 1):
                if ph > DEG:
                    pe.wait_ge(table_ready, ph)
                    for t in range(NT):
                        last = mm(bank[t // 4][0:FEAT, (t % 4) * P:(t % 4 + 1) * P], table[:, t, :], ident[:, :],
                                  start=True, stop=True)
                    last.then_inc(table_turned, 1)
                    pe.wait_ge(table_t_ready, ph)
                with pe.If(general < 1):
                    def step(c, s, users):
                        if ph == GCN1:
                            edge_mlp(c, s, users)
                        window_sums(ph, c, s, users)
                        if not isinstance(c, int) or c >= 1:
                            slot_sums(ph, c - 1, 1 - s)
                        if not isinstance(c, int) or c >= 2:
                            place_slots(ph, c - 2, s)
                    if ph == GRU1:
                        pe.wait_ge(hidden_ready, CHUNKS)
                    pe_steps(step)
                    slot_sums(ph, 74, 0)
                    place_slots(ph, 73, 1)
                    place_slots(ph, 74, 0)
                with pe.Else():
                    if ph == GCN1:
                        pe_steps(edge_mlp)
                        pe.wait_ge(hidden_ready, CHUNKS)
                    with pe.Fori(0, TILES) as t:
                        if ph >= GRU1:
                            pe.wait_ge(g_prod_ready, t + (1 + (ph - GRU1) * TILES))
                            pe.wait_ge(g_hidden_copied, t + (1 + (ph - GRU1) * TILES))
                            mm(bank[7][0:HIDDEN, 256:256 + P], g_hidden[:, :], ident[:, :],
                               start=True, stop=True).then_inc(g_transposed, 1)
                            pe.wait_ge(g_hidden_ready, t + (1 + (ph - GRU1) * TILES))
                            weights = bank[7][0:P, 0:FEAT * FEAT]
                            mm(weights, g_hidden_t[:, :], w2row[:, :], start=True, stop=False)
                            mm(weights, ones[0:1, :], b2row[:, :], start=False, stop=True).then_inc(g_weights, 1)
                            pe.wait_ge(g_msg_ready, t + (1 + (ph - GRU1) * TILES))
                        if ph > DEG:
                            pe.wait_ge(g_gathered[ph], t * 16 + 16)
                        what = ones[:, 0:FEAT] if ph == DEG else g_x[:, :] if ph <= GCN2 else g_msg[:, :]
                        pe.wait_ge(g_wide_ready, t + (1 + ph * TILES))
                        pe.wait_ge(g_added, t + (1 + ph * TILES))
                        for b in range(BLOCKS):
                            last = mm(bank[b][0:FEAT, 0:BLK], what, wide[:, b * BLK:(b + 1) * BLK], start=True, stop=True)
                        last.then_inc(g_blocks, 1)
                pe.nop()
                pe.wait_ge(node_free, ph + 1)
                if ph == DEG:
                    for t in range(NT):
                        last = mm(bank[7][0:P, t * FEAT:(t + 1) * FEAT], acc_view(t), ident[0:FEAT, 0:FEAT], start=True, stop=True)
                    last.then_inc(node_sums, 1)
                elif ph <= GCN2:
                    for t in range(NT):
                        to = bank[7][0:P, t * FEAT:(t + 1) * FEAT]
                        mm(to, acc_view(t), gw[ph - GCN1][:, :], start=True, stop=False)
                        last = mm(to, table_t[:, t * P:(t + 1) * P], gw[ph - GCN1][:, :], start=False, stop=True)
                    last.then_inc(node_sums, 1)
                else:
                    for t in range(NT):
                        at = slice((t % 10) * GATES, (t % 10 + 1) * GATES)
                        mm(bank[t // 10][0:P, at], acc_view(t), wih[:, :], start=True, stop=True)
                        last = mm(bank[3 + t // 10][0:P, at], table_t[:, t * P:(t + 1) * P], whh[:, :], start=True, stop=True)
                    last.then_inc(node_sums, 1)


def kernel(**inputs):
    import numpy as np
    import concourse.bacc as bacc
    from concourse.bass_utils import run_bass_kernel_spmd

    def flat(name, shape):
        return np.ascontiguousarray(np.asarray(inputs[name]).reshape(shape))

    def turned(name, shape):
        return np.ascontiguousarray(np.asarray(inputs[name]).reshape(shape).T)

    slot_matrix = np.concatenate([np.kron(np.eye(CH), np.ones((1, WIN))), np.tile(np.arange(WIN), (1, CH))])
    slot_matrix[0] -= 1
    arrays = {
        "x": flat("x", (NODES, FEAT)),
        "src": turned("src", (TILES, P)), "dst": turned("dst", (TILES, P)),
        "first": np.ascontiguousarray(np.asarray(inputs["dst"])[::P].reshape(CHUNKS, CH).T),
        "edge_t": turned("edge_attr_13", (EDGES, EDGE_FEAT)),
        "w1": flat("L1_gnn_fnet_w1", (EDGE_FEAT, HIDDEN)), "b1": flat("L1_gnn_fnet_b1", (1, HIDDEN)),
        "gw1": flat("L0_gnn_W1", (FEAT, FEAT)), "gb1": flat("L0_gnn_b1", (1, FEAT)),
        "gw2": flat("L0_gnn_W2", (FEAT, FEAT)), "gb2": flat("L0_gnn_b2", (1, FEAT)),
        "w2": flat("L1_gnn_fnet_w2", (HIDDEN, FEAT * FEAT)), "b2": flat("L1_gnn_fnet_b2", (1, FEAT * FEAT)),
        "wih_t": turned("L1_gnn_gru_w_ih", (GATES, FEAT)), "whh_t": turned("L1_gnn_gru_w_hh", (GATES, FEAT)),
        "bih": flat("L1_gnn_gru_b_ih", (1, GATES)), "bhh": flat("L1_gnn_gru_b_hh", (1, GATES)),
        "ident": np.eye(P, dtype=np.float32),
        "iota": np.tile(np.arange(BLK, dtype=np.float32), (P, 1)),
        "slot_matrix": slot_matrix.astype(np.float32),
    }
    nc = bacc.Bacc("TRN2", target_bir_lowering=False, num_devices=1)
    args = [nc.dram_tensor(f"in_{n}", a.shape, mybir.dt.from_np(a.dtype), kind="ExternalInput").ap()
            for n, a in arrays.items()]
    out = nc.dram_tensor("out", (NODES, FEAT), mybir.dt.float32, kind="ExternalOutput").ap()
    gnn_kernel(nc, *args, out)
    r = run_bass_kernel_spmd(nc, [{f"in_{n}": a for n, a in arrays.items()}], core_ids=[0])
    return r.results[0]["out"]
```

```python
import concourse.bass as bass
from concourse import mybir
from contextlib import ExitStack

NODES, FEAT, EDGES, EDGE_FEAT, HIDDEN = 3125, 16, 103125, 13, 32
P = 125
NT = NODES // P
TILES = EDGES // P
CH = 11
CHUNKS = TILES // CH
POOL_T = (0, 5, 5, 6, 6)
PE_MAX = CH - min(POOL_T[1:])
POOL_MAX = max(POOL_T)
KEYS, LOWS = 2, 13
HELD = KEYS * LOWS
ROWS = -(-NODES // HELD)
EC = PE_MAX * P
WIN = 8
SLOTS = CH * WIN
SPAN = 64
BLK = 456
BLOCKS = 7
ACCW = BLK * BLOCKS
BASE, TURN = 32, 64
GATES = 3 * FEAT
CW = CH * HIDDEN
XW = CH * WIN * FEAT
QUADS = 17
MLP_T = 6
MLP_ROWS = 1 + MLP_T * EDGE_FEAT
DEG, GCN1, GCN2, GRU1, GRU2 = range(5)


def gnn_kernel(nc, x_in, src_in, src_flat, keys_in, dst_in, first_in, edge_t, w1_in, b1_in, gw1_in, gb1_in, gw2_in, gb2_in,
               w2_in, b2_in, wih_t, whh_t, bih_in, bhh_in, ident_in, iota_in, slot_in, out):
    f32, i32, bf16, f16 = mybir.dt.float32, mybir.dt.int32, mybir.dt.bfloat16, mybir.dt.float16
    ALU, ACT, AX = mybir.AluOpType, mybir.ActivationFunctionType, mybir.AxisListType
    ds = bass.ds
    ctx = ExitStack()
    with ctx:
        def sb(name, shape, dt=f32):
            return ctx.enter_context(nc.sbuf_tensor(name, shape, dt))

        def sem(name):
            return ctx.enter_context(nc.semaphore(name))

        src_i = sb("src_i", [P, TILES], i32)
        dst_f = sb("dst_f", [P, TILES])
        onehot = sb("onehot", [P, TILES, WIN], bf16)
        hidden = sb("hidden", [P, TILES * HIDDEN])
        slot_node = sb("slot_node", [SLOTS, CHUNKS])
        ident = sb("ident", [P, P])
        iota = sb("iota", [P, BLK])
        ones = sb("ones", [P, P])
        ones_half = sb("ones_half", [P, FEAT], bf16)
        w2q = sb("w2q", [128, 4, FEAT])
        b2m = sb("b2m", [FEAT, FEAT])
        w2row = sb("w2row", [HIDDEN, FEAT * FEAT])
        gw = [sb("gw1", [FEAT, FEAT]), sb("gw2", [FEAT, FEAT])]
        gb = [sb("gb1", [P, FEAT]), sb("gb2", [P, FEAT])]
        wih = sb("wih", [FEAT, GATES])
        whh = sb("whh", [TURN + FEAT, GATES])[TURN:TURN + FEAT, :]
        gw_self = [sb(f"gw_self{k}", [TURN + FEAT, FEAT])[TURN:TURN + FEAT, :] for k in range(2)]
        bih = sb("bih", [P, GATES])
        bhh = sb("bhh", [P, GATES])
        keys = sb("keys", [ROWS, KEYS])
        low_hot = sb("low_hot", [P, CHUNKS * PE_MAX, LOWS], bf16)
        idx = [sb(f"idx{s}", [P, POOL_MAX], i32) for s in range(4)]
        xsrc = [sb(f"xsrc{s}", [P, CH, FEAT]) for s in range(4)]
        key_row = [sb(f"key_row{s}", [ROWS, EC], f16) for s in range(4)]
        key_hot = [sb(f"key_hot{s}", [ROWS, KEYS * EC + 128 - P], bf16) for s in range(2)]
        window = [sb(f"window{s}", [P, SLOTS]) for s in range(2)]
        hidden_ring = [sb(f"hidden_ring{s}", [P, CW]) for s in range(2)]
        sums_sb = [sb(f"sums_sb{s}", [128, CW]) for s in range(2)]
        xsum_sb = [sb(f"xsum_sb{s}", [FEAT, SLOTS]) for s in range(2)]
        slots_sb = [sb(f"slots_sb{s}", [SLOTS, FEAT]) for s in range(2)]
        place = [sb(f"place{s}", [SLOTS, SPAN]) for s in range(2)]
        first_i, first_f, slot_matrix = (hidden[0:CH + 1, (7 + k) * TILES:(7 + k) * TILES + w]
                                         for k, w in enumerate((CHUNKS, CHUNKS, SLOTS)))
        first_i = first_i[0:CH, :].bitcast(i32)
        dst_i = hidden[:, 6 * TILES:7 * TILES].bitcast(i32)
        low_f, key_f, key_p = (hidden[:, k * TILES:(k + 1) * TILES] for k in (2, 3, 4))
        key_f16 = hidden[:, 5 * TILES:6 * TILES].bitcast(f16)[:, 0:TILES]
        w1_blocks = key_row[0][0:MLP_ROWS, 0:2 * MLP_T * HIDDEN].bitcast(f32)
        scratch = sb("scratch", [P, 3 * NT * GATES])
        edges_sb = [scratch[0:MLP_ROWS, r * 2 * P:(r + 1) * 2 * P] for r in range(4)]
        xwin = [scratch[:, s * XW:(s + 1) * XW] for s in range(2)]
        wide = scratch[:, 0:ACCW]
        gate_i, gate_h, gate_n = (scratch[:, k * NT * GATES:(k + 1) * NT * GATES]
                                  .rearrange("p (t g) -> p t g", g=GATES) for k in range(3))
        rows = sb("rows", [TURN + FEAT, ACCW])
        acc = rows[0:FEAT, :]
        table_t = rows[TURN:TURN + FEAT, 0:NODES]
        first_dst = rows[BASE:BASE + 1, 0:TILES].bitcast(i32)
        b2row = rows[BASE:BASE + 1, TILES:TILES + FEAT * FEAT]
        x0 = sb("x0", [P, NT, FEAT])
        x1 = sb("x1", [P, NT, FEAT])
        table = sb("table", [P, NT, FEAT])
        parts = sb("parts", [ROWS, 3, HELD * FEAT], bf16)
        picked = sb("picked", [P, PE_MAX * LOWS, FEAT])
        held, left = (picked[0:ROWS, k * HELD:(k + 1) * HELD, :].rearrange("p t f -> p (t f)") for k in range(2))
        y = sb("y", [P, NT, FEAT])
        z = picked[:, 2 * HELD:2 * HELD + NT, :]
        dinv = sb("dinv", [P, NT, 1])
        inv_deg = sb("inv_deg", [P, NT, 1])
        stat = sb("stat", [P, NT, 1])
        var = sb("var", [P, NT, 1])
        worst = sb("worst", [P, 4])
        flag_f = sb("flag_f", [1, 1])
        flag_i = sb("flag_i", [1, 1], i32)
        g_idx = sb("g_idx", [P, 1], i32)
        g_x = sb("g_x", [P, FEAT])
        g_hidden = hidden_ring[1][:, 0:HIDDEN]
        g_hidden_t = hidden_ring[0][0:HIDDEN, 0:P]
        g_prod = picked[:, 0:FEAT, :]
        g_msg = sb("g_msg", [P, FEAT])

        bank = [ctx.enter_context(nc.psum_tensor(f"bank{i}", [128, 512], f32)) for i in range(8)]
        sum_bank, slot_bank, place_bank, pick_bank, mlp_bank = bank[0:2], bank[2], bank[3], bank[4:8], bank[6:8]

        tables = [None] + [nc.dram_tensor(f"table_dram{k}", [NODES, FEAT], f32).ap() for k in range(1, 5)]
        keys_dram = nc.dram_tensor("keys_dram", [P, TILES], f16).ap()
        keys_flat = keys_dram.rearrange("(o p) t -> o (p t)", o=1)

        ints_in = sem("ints_in")
        consts_in = sem("consts_in")
        edges_in = [sem(f"edges_in{r}") for r in range(4)]
        w1_zero = sem("w1_zero")
        w1_in_place = sem("w1_in_place")
        dst_ready = sem("dst_ready")
        bases_ready = sem("bases_ready")
        flags_sum = sem("flags_sum")
        flag_ready = sem("flag_ready")
        v_step = sem("v_step")
        onehot_ready = sem("onehot_ready")
        acc_zero = sem("acc_zero")
        idx_ready = sem("idx_ready")
        gather_turn = sem("gather_turn")
        load_turn = sem("load_turn")
        gathered = [None] + [[sem(f"gathered{k}_{s}") for s in range(4)] for k in range(1, 5)]
        ones_set = sem("ones_set")
        keys_made = sem("keys_made")
        keys_stored = sem("keys_stored")
        key_row_in = [sem(f"key_row_in{s}") for s in range(4)]
        key_hot_ready = sem("key_hot_ready")
        held_in = sem("held_in")
        parts_ready = sem("parts_ready")
        pick_done = sem("pick_done")
        picked_low = sem("picked_low")
        xsrc_ready = sem("xsrc_ready")
        xwin_ready = sem("xwin_ready")
        place_ready = sem("place_ready")
        summed = sem("summed")
        window_copied = sem("window_copied")
        xsum_copied = sem("xsum_copied")
        slotted = sem("slotted")
        slots_copied = sem("slots_copied")
        placed = sem("placed")
        added = sem("added")
        mlp_done = sem("mlp_done")
        hidden_ready = sem("hidden_ready")
        hidden_copied = sem("hidden_copied")
        g_idx_ready = sem("g_idx_ready")
        g_gathered = [None] + [sem(f"g_gathered{k}") for k in range(1, 5)]
        g_hidden_copied = sem("g_hidden_copied")
        g_transposed = sem("g_transposed")
        g_hidden_ready = sem("g_hidden_ready")
        g_weights = sem("g_weights")
        g_prod_ready = sem("g_prod_ready")
        g_msg_ready = sem("g_msg_ready")
        g_wide_ready = sem("g_wide_ready")
        g_blocks = sem("g_blocks")
        g_added = sem("g_added")
        table_ready = sem("table_ready")
        table_stored = sem("table_stored")
        table_turned = sem("table_turned")
        table_t_ready = sem("table_t_ready")
        node_sums = sem("node_sums")
        node_hidden = sem("node_hidden")
        node_free = sem("node_free")
        rz_in = sem("rz_in")
        rz_out = sem("rz_out")
        n_in = sem("n_in")
        n_out = sem("n_out")
        sqrt_in = sem("sqrt_in")
        sqrt_out = sem("sqrt_out")
        out_ready = sem("out_ready")
        out_stored = sem("out_stored")

        N_CONSTS = 21
        SLOT_USES = [len(range(r, CHUNKS, 4)) for r in range(4)]
        ROOTS = (DEG, GCN2, GRU2)

        def steps(eng, step):
            for c in range(4):
                step(c, c % 2, c % 4, c // 4 + 1)
            with nc.Fori(0, QUADS, engines=[eng.engine], hint_back_edge=True) as i:
                for k in range(4, 8):
                    step(i * 4 + k, k % 2, k % 4, i + (k // 4 + 1))
            for c in (72, 73, 74):
                step(c, c % 2, c % 4, c // 4 + 1)

        def later(c, n):
            return not isinstance(c, int) or c >= n

        def within(c, ahead):
            return not isinstance(c, int) or c + ahead < CHUNKS

        def acc_view(t):
            return acc[:, 0:NODES].rearrange("f (p t) -> f t p", t=NT)[:, t, :]

        block = ctx.enter_context(nc.Block())

        @block.sync
        def _(sp):
            sp.dma_start(dst_i, dst_in).then_inc(ints_in, 16)
            sp.dma_start(first_i, first_in).then_inc(ints_in, 16)
            sp.dma_start(first_dst, dst_in[0:1, :]).then_inc(ints_in, 16)
            sp.dma_start(src_i[:, :], src_in).then_inc(ints_in, 16)
            sp.dma_start(low_f.bitcast(i32), src_flat).then_inc(ints_in, 16)
            loads = [(ident[:, :], ident_in), (iota[:, :], iota_in), (keys[:, :], keys_in), (slot_matrix, slot_in),
                     (x0[:, :, :], x_in.rearrange("(p t) f -> p t f", t=NT)),
                     (b2m[:, :], b2_in.rearrange("a (i o) -> (a i) o", o=FEAT)), (b2row, b2_in),
                     (w2row[:, :], w2_in), (gw[0][:, :], gw1_in), (gw[1][:, :], gw2_in),
                     (wih[:, :], wih_t), (whh, whh_t),
                     (gw_self[0], gw1_in), (gw_self[1], gw2_in)]
            loads += [(w2q[q * HIDDEN:(q + 1) * HIDDEN, :, :],
                       w2_in[:, q * 64:(q + 1) * 64].rearrange("k (i o) -> k i o", o=FEAT)) for q in range(4)]
            loads += [(gb[0][:, :], gb1_in.to_broadcast([P, FEAT])), (gb[1][:, :], gb2_in.to_broadcast([P, FEAT])),
                      (bih[:, :], bih_in.to_broadcast([P, GATES])), (bhh[:, :], bhh_in.to_broadcast([P, GATES]))]
            assert len(loads) == N_CONSTS + 1
            for to, what in loads:
                sp.dma_start(to, what).then_inc(consts_in, 16)

            sp.wait_ge(w1_zero, 1)
            for j in range(MLP_T):
                at = slice(j * HIDDEN, (j + 1) * HIDDEN)
                sp.dma_start(w1_blocks[1 + j * EDGE_FEAT:1 + (j + 1) * EDGE_FEAT, at], w1_in).then_inc(w1_in_place, 16)
                sp.dma_start(w1_blocks[0:1, at], b1_in).then_inc(w1_in_place, 16)
            sp.wait_ge(keys_made, 1)
            sp.dma_start(keys_dram, key_f16).then_inc(keys_stored, 16)
            sp.wait_ge(keys_stored, 16)

            def load_keys(ph, c, r):
                if later(c, 4):
                    sp.wait_ge(key_hot_ready, c + ((ph - GCN1) * CHUNKS - 3))
                    sp.sem_inc(load_turn, 1)
                w = (CH - POOL_T[ph]) * P
                sp.dma_start(key_row[r][:, 0:w], keys_flat[:, ds(c * (CH * P) + POOL_T[ph] * P, w)].to_broadcast([ROWS, w])
                             ).then_inc(key_row_in[r], 16)

            def load_edges(c, s, r, n):
                if later(c, 4):
                    sp.wait_ge(mlp_done, c - 3)
                    sp.sem_inc(load_turn, 1)
                sp.dma_start(edges_sb[r][1:MLP_ROWS, :], edge_t[:, ds(c * (2 * P), 2 * P)]).then_inc(edges_in[r], 16)

            sp.wait_ge(flag_ready, 1)
            general = sp.value_load(flag_i[0:1, 0:1], min_val=0, max_val=1)
            steps(sp, load_edges)
            for k in range(1, 5):
                sp.wait_ge(table_ready, k)
                sp.dma_start(tables[k].rearrange("(p t) f -> p t f", t=NT), table[:, :, :]).then_inc(table_stored, 16)
                sp.wait_ge(table_stored, 16 * k)
                whole = ROWS - 1
                sp.dma_start(held[0:whole, :], tables[k][0:whole * HELD, :].rearrange("(p t) f -> p (t f)", t=HELD)
                             ).then_inc(held_in, 16)
                rest = (NODES - whole * HELD) * FEAT
                sp.dma_start(held[whole:ROWS, 0:rest], tables[k][whole * HELD:NODES, :].rearrange("(o t) f -> o (t f)", o=1)
                             ).then_inc(held_in, 16)

                def step(c, s, r, n):
                    if within(c, 2):
                        load_keys(k, c + 2, (r + 2) % 4)

                with sp.If(general < 1):
                    load_keys(k, 0, 0)
                    load_keys(k, 1, 1)
                    steps(sp, step)
                sp.nop()
            sp.wait_ge(table_stored, 64)
            sp.wait_ge(out_ready, 1)
            sp.dma_start(out.rearrange("(p t) f -> p t f", t=NT), y[:, :, :]).then_inc(out_stored, 16)
            sp.wait_ge(out_stored, 16)

        @block.gpsimd
        def _(pool):
            pool.wait_ge(flag_ready, 1)
            general = pool.value_load(flag_i[0:1, 0:1], min_val=0, max_val=1)
            for ph in range(GCN1, GRU2 + 1):
                pool.wait_ge(table_stored, 16 * ph)
                with pool.If(general < 1):
                    def gather(c, s, r, n):
                        pool.wait_ge(idx_ready, c + (1 + (ph - 1) * CHUNKS))
                        if later(c, 4):
                            pool.wait_ge(summed, c + (ph * CHUNKS - 3))
                        pool.sem_inc(gather_turn, 1)
                        for j in range(POOL_T[ph]):
                            pool.indirect_dma_start(
                                out=xsrc[r][:, j, :], out_offset=None, in_=tables[ph],
                                in_offset=bass.IndirectOffsetOnAxis(ap=idx[r][:, j:j + 1], axis=0)
                            ).then_inc(gathered[ph][r], 16)
                    steps(pool, gather)
                with pool.Else():
                    with pool.Fori(0, TILES) as t:
                        pool.wait_ge(g_idx_ready, t + (1 + (ph - 1) * TILES))
                        pool.sem_inc(gather_turn, 1)
                        pool.indirect_dma_start(
                            out=g_x[:, :], out_offset=None, in_=tables[ph],
                            in_offset=bass.IndirectOffsetOnAxis(ap=g_idx[:, 0:1], axis=0)
                        ).then_inc(g_gathered[ph], 16)
                pool.nop()

        @block.scalar
        def _(act):
            act.wait_ge(flag_ready, 1)
            act.wait_ge(onehot_ready, 1)
            act.wait_ge(keys_stored, 16)
            general = act.value_load(flag_i[0:1, 0:1], min_val=0, max_val=1)

            def relu_hidden(c, s, r, n):
                act.wait_ge(mlp_done, c + 1)
                nc.scalar.activation(hidden[:, ds(c * CW, CW)], mlp_bank[s][0:P, 0:CW], ACT.Relu).then_inc(hidden_ready, 1)

            def copy_hidden(ph, c, s):
                if later(c, 2):
                    act.wait_ge(summed, c + (ph * CHUNKS - 1))
                nc.scalar.activation(hidden_ring[s][:, :], hidden[:, ds(c * CW, CW)], ACT.Copy).then_inc(hidden_copied, 1)

            def copy_window(ph, c, s):
                if later(c, 2):
                    act.wait_ge(summed, c + (ph * CHUNKS - 1))
                nc.scalar.activation(window[s][:, :].rearrange("p (j n) -> p j n", n=WIN), onehot[:, ds(c * CH, CH), :], ACT.Copy
                                     ).then_inc(window_copied, 1)

            def copy_sums(ph, c, s):
                act.wait_ge(summed, c + (1 + ph * CHUNKS))
                if later(c, 2):
                    act.wait_ge(slotted, c + (ph * CHUNKS - 1))
                if ph >= GRU1:
                    nc.scalar.activation(sums_sb[s][:, :], sum_bank[s][:, 0:CW], ACT.Copy)
                nc.scalar.activation(xsum_sb[s][:, :], sum_bank[s][0:FEAT, CW:CW + SLOTS], ACT.Copy).then_inc(xsum_copied, 1)

            def copy_slots(ph, c, s):
                act.wait_ge(slotted, c + (1 + ph * CHUNKS))
                if later(c, 2):
                    act.wait_ge(placed, c + (ph * CHUNKS - 1))
                nc.scalar.activation(slots_sb[s][:, :], slot_bank[0:SLOTS, 0:FEAT], ACT.Copy).then_inc(slots_copied, 1)

            for ph in range(DEG, GRU2 + 1):
                if ph == GRU1:
                    act.wait_ge(hidden_ready, CHUNKS)
                if ph > DEG:
                    act.wait_ge(table_turned, ph)
                    for b in range(7):
                        w = min(4, NT - 4 * b) * P
                        last = nc.scalar.activation(table_t[:, 4 * b * P:4 * b * P + w], bank[b][0:FEAT, 0:w], ACT.Copy)
                    last.then_inc(table_t_ready, 1)
                with act.If(general < 1):
                    def step(c, s, r, n):
                        if ph > DEG:
                            copy_window(ph, c, s)
                        if ph >= GRU1:
                            copy_hidden(ph, c, s)
                        copy_sums(ph, c, s)
                        if ph == DEG:
                            relu_hidden(c, s, r, n)
                        if later(c, 1):
                            copy_slots(ph, c - 1, 1 - s)
                    steps(act, step)
                    copy_slots(ph, CHUNKS - 1, 0)
                with act.Else():
                    if ph == DEG:
                        steps(act, relu_hidden)
                    if ph >= GRU1:
                        with act.Fori(0, TILES) as t:
                            act.wait_ge(g_transposed, t + (2 + (ph - GRU1) * TILES))
                            nc.scalar.activation(g_hidden_t, bank[7][0:HIDDEN, 256:256 + P], ACT.Copy).then_inc(g_hidden_ready, 1)
                act.nop()
                if ph >= GRU1:
                    act.wait_ge(rz_in, ph - GRU1 + 1)
                    nc.scalar.activation(gate_i[:, :, 0:32], gate_i[:, :, 0:32], ACT.Sigmoid).then_inc(rz_out, 1)
                    act.wait_ge(n_in, ph - GRU1 + 1)
                    nc.scalar.activation(gate_n[:, :, 0:16], gate_n[:, :, 0:16], ACT.Tanh).then_inc(n_out, 1)
                if ph in ROOTS:
                    act.wait_ge(sqrt_in, ROOTS.index(ph) + 1)
                    nc.scalar.activation(var[:, :, :], var[:, :, :], ACT.Sqrt).then_inc(sqrt_out, 1)

        @block.vector
        def _(dve):
            chained = [0]

            def link(ins):
                chained[0] += 1
                ins.then_inc(v_step, 1)
                dve.wait_ge(v_step, chained[0])

            for free in (g_blocks, g_added, g_transposed, g_prod_ready):
                dve.sem_inc(free, 1)
            nc.vector.memset(ones[:, :], 1.0)
            nc.vector.memset(ones_half[:, :], 1.0)
            nc.vector.memset(w1_blocks, 0.0).then_inc(w1_zero, 1)
            nc.vector.memset(scratch[0:1, 0:4 * 2 * P], 1.0).then_inc(ones_set, 1)
            for s in range(2):
                nc.vector.memset(key_hot[s][:, :], 0.0)
            link(nc.vector.memset(first_f, 1.0))
            dve.wait_ge(ints_in, 80)
            nc.vector.tensor_copy(first_f[0:CH, :], first_i)
            nc.vector.tensor_copy(dst_f[:, :], dst_i).then_inc(dst_ready, 1)
            dve.wait_ge(dst_ready, 1)
            dve.wait_ge(consts_in, 16 * (N_CONSTS + 1))
            for src, twice in ((low_f.bitcast(i32), key_f), (src_i[:, :], key_p)):
                link(nc.vector.tensor_copy(twice, src))
                link(nc.vector.tensor_scalar(twice, twice, -float(LOWS // 2), 1.0 / LOWS, ALU.add, ALU.mult))
                link(nc.vector.tensor_scalar(twice, twice, 12582912.0, None, ALU.add))
                link(nc.vector.tensor_scalar(twice, twice, -12582912.0, None, ALU.add))
            nc.vector.tensor_copy(key_f16, key_f).then_inc(keys_made, 1)
            link(nc.vector.tensor_copy(low_f, src_i[:, :]))
            link(nc.vector.scalar_tensor_tensor(low_f, key_p, -float(LOWS), low_f, ALU.mult, ALU.add))
            lows = low_f.rearrange("p (c j) -> p c j", j=CH)
            for j in range(PE_MAX):
                at = low_hot[:, :, :].rearrange("p (c j) w -> p c j w", j=PE_MAX)[:, :, j, :]
                of = lows[:, :, CH - PE_MAX + j:CH - PE_MAX + j + 1].to_broadcast([P, CHUNKS, LOWS])
                last = nc.vector.tensor_tensor(at, of, iota[:, 0:LOWS].rearrange("p (o w) -> p o w", o=1)
                                               .to_broadcast([P, CHUNKS, LOWS]), ALU.is_equal)
            link(last)
            dve.wait_ge(bases_ready, 1)
            half = 35 * CH
            rel = hidden[:, 0:TILES]
            from_chunk = hidden[:, TILES:2 * TILES]
            for n0, n1, b in ((0, half, 0), (half, TILES, 1)):
                base = bank[b][0:P, 0:n1 - n0]
                nc.vector.tensor_tensor(rel[:, n0:n1], dst_f[:, n0:n1], base, ALU.subtract)
                chunk_base = base.rearrange("p (c j) -> p c j", j=CH)[:, :, 0:1].to_broadcast([P, (n1 - n0) // CH, CH])
                last = nc.vector.tensor_tensor(from_chunk[:, n0:n1].rearrange("p (c j) -> p c j", j=CH),
                                               dst_f[:, n0:n1].rearrange("p (c j) -> p c j", j=CH), chunk_base, ALU.subtract)
            link(last)
            nc.vector.tensor_copy(slot_node[:, :], bank[2][0:SLOTS, 0:CHUNKS])
            nc.vector.tensor_tensor(onehot[:, :, :], rel.rearrange("p (t o) -> p t o", o=1).to_broadcast([P, TILES, WIN]),
                                    iota[:, 0:WIN].rearrange("p (o w) -> p o w", o=1).to_broadcast([P, TILES, WIN]),
                                    ALU.is_equal).then_inc(onehot_ready, 1)
            nc.vector.tensor_reduce(worst[:, 0:1], rel, AX.X, ALU.max)
            nc.vector.tensor_reduce(worst[:, 1:2], from_chunk, AX.X, ALU.max)
            nc.vector.tensor_reduce(worst[:, 2:3], rel, AX.X, ALU.min)
            link(nc.vector.tensor_reduce(worst[:, 3:4], from_chunk, AX.X, ALU.min))
            nc.vector.tensor_scalar(worst[:, 0:1], worst[:, 0:1], float(WIN), None, ALU.is_ge)
            nc.vector.tensor_scalar(worst[:, 1:2], worst[:, 1:2], float(SPAN), None, ALU.is_ge)
            link(nc.vector.tensor_scalar(worst[:, 2:4], worst[:, 2:4], 0.0, None, ALU.is_lt))
            link(nc.vector.tensor_reduce(var[:, 0, :], worst[:, :], AX.X, ALU.max))
            nc.vector.tensor_copy(stat[:, 0, :], var[:, 0, :]).then_inc(flags_sum, 1)
            dve.wait_ge(flags_sum, 2)
            link(nc.vector.tensor_scalar(flag_f[:, :], bank[3][0:1, 0:1], 0.5, None, ALU.is_ge))
            link(nc.vector.tensor_copy(flag_i[:, :], flag_f[:, :]))
            dve.nop().then_inc(flag_ready, 1)
            general = dve.value_load(flag_i[0:1, 0:1], min_val=0, max_val=1)

            def window_first(c):
                return dve.value_load(first_dst[0:1, ds(c * CH, 1)], min_val=0, max_val=NODES - 1)

            def add_placed(ph, c, s, first):
                dve.wait_ge(placed, c + (1 + ph * CHUNKS))
                if later(c, 1):
                    dve.wait_ge(added, c + ph * CHUNKS)
                nodes = acc[:, ds(first, SPAN)]
                nc.vector.tensor_tensor(nodes, nodes, place_bank[0:FEAT, 0:SPAN], ALU.add).then_inc(added, 1)

            def take_idx(ph, c, r, n):
                if later(c, 4):
                    dve.wait_ge(gathered[ph][r], (n - 1) * (16 * POOL_T[ph]))
                nc.vector.tensor_copy(idx[r][:, 0:POOL_T[ph]], src_i[:, ds(c * CH, POOL_T[ph])]).then_inc(idx_ready, 1)

            def make_key_hot(ph, c, s, r, n):
                dve.wait_ge(key_row_in[r], (n + (ph - GCN1) * SLOT_USES[r]) * 16)
                if later(c, 2):
                    dve.wait_ge(pick_done, c + ((ph - GCN1) * CHUNKS - 1))
                w = (CH - POOL_T[ph]) * P
                for a in range(KEYS):
                    last = nc.vector.tensor_scalar(key_hot[s][:, a * EC:a * EC + w], key_row[r][:, 0:w], keys[:, a:a + 1], None, ALU.is_equal)
                last.then_inc(key_hot_ready, 1)

            def pick_low(ph, c, s, r):
                dve.wait_ge(pick_done, c + (1 + (ph - GCN1) * CHUNKS))
                if later(c, 4):
                    dve.wait_ge(summed, c + (ph * CHUNKS - 3))
                if later(c, 1):
                    dve.wait_ge(xsrc_ready, c + (ph - GCN1) * CHUNKS)
                mine = CH - POOL_T[ph]
                for j in range(0, mine, 2):
                    m = min(2, mine - j) * LOWS
                    low = low_hot[:, ds(c * PE_MAX + (PE_MAX - mine + j), m // LOWS), :]
                    last = nc.vector.tensor_tensor(
                        picked[:, j * LOWS:j * LOWS + m, :], pick_bank[j // 2][0:P, 0:m * FEAT].rearrange("p (m f) -> p m f", f=FEAT),
                        low.rearrange("p j (b o) -> p (j b) o", o=1).to_broadcast([P, m, FEAT]), ALU.mult)
                last.then_inc(picked_low, 1)
                dve.wait_ge(picked_low, c + (1 + (ph - GCN1) * CHUNKS))
                nc.vector.tensor_reduce(xsrc[r][:, POOL_T[ph]:CH, :],
                                        picked[:, 0:mine * LOWS, :].rearrange("p (j b) f -> p j f b", b=LOWS),
                                        AX.X, ALU.add).then_inc(xsrc_ready, 1)

            def split_table(ph):
                dve.wait_ge(held_in, 32 * ph)
                link(nc.vector.tensor_copy(parts[:, 0, :], held))
                link(nc.vector.tensor_tensor(left, held, parts[:, 0, :], ALU.subtract))
                link(nc.vector.tensor_copy(parts[:, 1, :], left))
                link(nc.vector.tensor_tensor(left, left, parts[:, 1, :], ALU.subtract))
                nc.vector.tensor_copy(parts[:, 2, :], left).then_inc(parts_ready, 1)

            def make_place(ph, c, s):
                if later(c, 2):
                    dve.wait_ge(placed, c + (ph * CHUNKS - 1))
                nc.vector.tensor_scalar(place[s][:, :], iota[0:SLOTS, 0:SPAN], slot_node[:, ds(c, 1)], None,
                                        ALU.is_equal).then_inc(place_ready, 1)

            def widen(ph, c, s, r, n):
                dve.wait_ge(gathered[ph][r], n * (16 * POOL_T[ph]))
                if ph >= GRU1:
                    dve.wait_ge(xsrc_ready, c + (1 + (ph - GCN1) * CHUNKS))
                    if later(c, 2):
                        dve.wait_ge(summed, c + (ph * CHUNKS - 1))
                    nc.vector.tensor_tensor(
                        xwin[s].rearrange("p (j n i) -> p j n i", n=WIN, i=FEAT),
                        xsrc[r][:, :, :].rearrange("p j (o i) -> p j o i", o=1).to_broadcast([P, CH, WIN, FEAT]),
                        onehot[:, ds(c * CH, CH), :].rearrange("p j (n o) -> p j n o", o=1).to_broadcast([P, CH, WIN, FEAT]),
                        ALU.mult).then_inc(xwin_ready, 1)

            def normalise(to, turn):
                link(nc.vector.tensor_reduce(stat[:, :, :], y[:, :, :], AX.X, ALU.add))
                link(nc.vector.tensor_scalar(stat[:, :, :], stat[:, :, :], 1.0 / FEAT, None, ALU.mult))
                link(nc.vector.tensor_tensor(y[:, :, :], y[:, :, :], stat[:, :, :].to_broadcast([P, NT, FEAT]), ALU.subtract))
                link(nc.vector.tensor_tensor(z[:, :, :], y[:, :, :], y[:, :, :], ALU.mult))
                link(nc.vector.tensor_reduce(var[:, :, :], z[:, :, :], AX.X, ALU.add))
                nc.vector.tensor_scalar(var[:, :, :], var[:, :, :], 1.0 / FEAT, 1e-5, ALU.mult, ALU.add).then_inc(sqrt_in, 1)
                dve.wait_ge(sqrt_out, turn)
                link(nc.vector.reciprocal(var[:, :, :], var[:, :, :]))
                return nc.vector.tensor_tensor(to, y[:, :, :], var[:, :, :].to_broadcast([P, NT, FEAT]), ALU.mult)

            for ph in range(DEG, GRU2 + 1):
                if ph > DEG:
                    split_table(ph)
                link(nc.vector.memset(acc[:, :], 0.0))
                with dve.If(general < 1):
                    def step(c, s, r, n):
                        if ph > DEG and within(c, 2):
                            make_key_hot(ph, c + 2, s, (r + 2) % 4, n + (r + 2) // 4)
                        if later(c, 3):
                            add_placed(ph, c - 3, 1 - s, window_first(c - 3))
                        if ph > DEG:
                            if within(c, 3):
                                take_idx(ph, c + 3, (r + 3) % 4, n + (r + 3) // 4)
                            widen(ph, c, s, r, n)
                        if later(c, 1):
                            make_place(ph, c - 1, 1 - s)
                        if ph > DEG and within(c, 1):
                            pick_low(ph, c + 1, 1 - s, (r + 1) % 4)
                    if ph > DEG:
                        for c in range(3):
                            take_idx(ph, c, c, 1)
                        make_key_hot(ph, 0, 0, 0, 1)
                        make_key_hot(ph, 1, 1, 1, 1)
                        pick_low(ph, 0, 0, 0)
                    steps(dve, step)
                    make_place(ph, 74, 0)
                    for c in (72, 73, 74):
                        add_placed(ph, c, c % 2, window_first(c))
                    dve.wait_ge(added, (ph + 1) * CHUNKS)
                with dve.Else():
                    if ph == DEG:
                        dve.wait_ge(mlp_done, CHUNKS)
                    with dve.Fori(0, TILES) as t:
                        if ph > DEG:
                            dve.wait_ge(g_blocks, t + (1 + ph * TILES))
                            nc.vector.tensor_copy(g_idx[:, :], src_i[:, ds(t, 1)]).then_inc(g_idx_ready, 1)
                        if ph >= GRU1:
                            dve.wait_ge(g_transposed, t + (1 + (ph - GRU1) * TILES))
                            nc.vector.tensor_copy(g_hidden, hidden[:, ds(t * HIDDEN, HIDDEN)]).then_inc(g_hidden_copied, 1)
                        dve.wait_ge(g_blocks, t + (1 + ph * TILES))
                        for b in range(BLOCKS):
                            last = nc.vector.tensor_scalar(wide[:, b * BLK:(b + 1) * BLK], iota[:, :], float(b * BLK),
                                                           dst_f[:, ds(t, 1)], ALU.add, ALU.is_equal)
                        last.then_inc(g_wide_ready, 1)
                        if ph > DEG:
                            dve.wait_ge(g_gathered[ph], t * 16 + 16)
                        if ph >= GRU1:
                            dve.wait_ge(g_weights, t + (1 + (ph - GRU1) * TILES))
                            nc.vector.tensor_tensor(g_prod, bank[7][0:P, 0:FEAT * FEAT].rearrange("p (i o) -> p i o", o=FEAT),
                                                    g_x[:, :].rearrange("p (i o) -> p i o", o=1).to_broadcast([P, FEAT, FEAT]),
                                                    ALU.mult).then_inc(g_prod_ready, 1)
                            dve.wait_ge(g_prod_ready, t + (2 + (ph - GRU1) * TILES))
                            nc.vector.tensor_reduce(g_msg[:, :], g_prod.rearrange("p i o -> p o i"), AX.X, ALU.add).then_inc(g_msg_ready, 1)
                        dve.wait_ge(g_blocks, t + (2 + ph * TILES))
                        dve.wait_ge(g_added, t + (1 + ph * TILES))
                        for b in range(BLOCKS):
                            part = acc[:, b * BLK:(b + 1) * BLK]
                            last = nc.vector.tensor_tensor(part, part, bank[b][0:FEAT, 0:BLK], ALU.add)
                        last.then_inc(g_added, 1)
                    dve.wait_ge(g_added, 1 + (ph + 1) * TILES)
                if ph < GRU2:
                    link(nc.vector.memset(held, 0.0))
                dve.nop().then_inc(node_free, 1)
                dve.wait_ge(node_sums, ph + 1)
                if ph == DEG:
                    count = bank[7][0:P, 0:NT * FEAT].rearrange("p (t f) -> p t f", f=FEAT)[:, :, 0:1]
                    nc.vector.tensor_scalar(stat[:, :, :], count, 1.0, None, ALU.max)
                    nc.vector.tensor_scalar(var[:, :, :], count, 1.0, None, ALU.add).then_inc(sqrt_in, 1)
                    dve.wait_ge(sqrt_out, 1)
                    link(nc.vector.reciprocal(dinv[:, :, :], var[:, :, :]))
                    link(nc.vector.reciprocal(inv_deg[:, :, :], stat[:, :, :]))
                    nc.vector.tensor_tensor(table[:, :, :], x0[:, :, :], dinv[:, :, :].to_broadcast([P, NT, FEAT]),
                                            ALU.mult).then_inc(table_ready, 1)
                elif ph <= GCN2:
                    edges_part, self_part = (bank[b][0:P, 0:NT * FEAT].rearrange("p (t f) -> p t f", f=FEAT) for b in (7, 6))
                    link(nc.vector.tensor_copy(y[:, :, :], edges_part))
                    link(nc.vector.tensor_tensor(y[:, :, :], y[:, :, :], self_part, ALU.add))
                    link(nc.vector.tensor_tensor(y[:, :, :], y[:, :, :], dinv[:, :, :].to_broadcast([P, NT, FEAT]), ALU.mult))
                    link(nc.vector.tensor_tensor(y[:, :, :], y[:, :, :], gb[ph - GCN1][:, :].rearrange("p (o f) -> p o f", o=1)
                                                 .to_broadcast([P, NT, FEAT]), ALU.add))
                    dve.wait_ge(table_stored, 16 * ph)
                    dve.wait_ge(table_turned, ph)
                    if ph == GCN1:
                        link(nc.vector.tensor_scalar(y[:, :, :], y[:, :, :], 0.0, None, ALU.max))
                        nc.vector.tensor_tensor(table[:, :, :], y[:, :, :], dinv[:, :, :].to_broadcast([P, NT, FEAT]),
                                                ALU.mult).then_inc(table_ready, 1)
                    else:
                        link(nc.vector.tensor_tensor(y[:, :, :], y[:, :, :], x0[:, :, :], ALU.add))
                        link(normalise(x1[:, :, :], 2))
                        nc.vector.tensor_copy(table[:, :, :], x1[:, :, :]).then_inc(table_ready, 1)
                else:
                    def wide3(ap, w):
                        return ap.to_broadcast([P, NT, w])

                    def bias(ap, w):
                        return ap.rearrange("p (o g) -> p o g", o=1).to_broadcast([P, NT, w])
                    for b in range(3):
                        t0, t1 = 10 * b, min(10 * b + 10, NT)
                        w = (t1 - t0) * GATES
                        nc.vector.tensor_tensor(gate_i[:, t0:t1, :], bank[b][0:P, 0:w].rearrange("p (t g) -> p t g", g=GATES),
                                                inv_deg[:, t0:t1, :].to_broadcast([P, t1 - t0, GATES]), ALU.mult)
                        last = nc.vector.tensor_tensor(gate_h[:, t0:t1, :], bank[3 + b][0:P, 0:w].rearrange("p (t g) -> p t g", g=GATES),
                                                       bhh[:, :].rearrange("p (o g) -> p o g", o=1).to_broadcast([P, t1 - t0, GATES]), ALU.add)
                    link(last)
                    link(nc.vector.tensor_tensor(gate_i[:, :, :], gate_i[:, :, :], bias(bih[:, :], GATES), ALU.add))
                    nc.vector.tensor_tensor(gate_i[:, :, 0:32], gate_i[:, :, 0:32], gate_h[:, :, 0:32], ALU.add).then_inc(rz_in, 1)
                    dve.wait_ge(rz_out, ph - GRU1 + 1)
                    link(nc.vector.tensor_tensor(gate_n[:, :, 0:16], gate_i[:, :, 0:16], gate_h[:, :, 32:48], ALU.mult))
                    nc.vector.tensor_tensor(gate_n[:, :, 0:16], gate_n[:, :, 0:16], gate_i[:, :, 32:48], ALU.add).then_inc(n_in, 1)
                    dve.wait_ge(n_out, ph - GRU1 + 1)
                    link(nc.vector.tensor_tensor(y[:, :, :], table[:, :, :], gate_n[:, :, 0:16], ALU.subtract))
                    link(nc.vector.tensor_tensor(y[:, :, :], y[:, :, :], gate_i[:, :, 16:32], ALU.mult))
                    link(nc.vector.tensor_tensor(y[:, :, :], y[:, :, :], gate_n[:, :, 0:16], ALU.add))
                    if ph == GRU1:
                        dve.wait_ge(table_stored, 16 * ph)
                        dve.wait_ge(table_turned, ph)
                        nc.vector.tensor_copy(table[:, :, :], y[:, :, :]).then_inc(table_ready, 1)
                    else:
                        link(nc.vector.tensor_tensor(y[:, :, :], y[:, :, :], x1[:, :, :], ALU.add))
                        link(normalise(z[:, :, :], 3))
                        nc.vector.tensor_copy(y[:, :, :], z[:, :, :]).then_inc(out_ready, 1)

        @block.tensor
        def _(pe):
            mm = nc.tensor.matmul
            pe.wait_ge(dst_ready, 1)
            pe.wait_ge(consts_in, 16 * (N_CONSTS + 1))
            half = 35 * CH
            mm(bank[0][0:P, 0:half], ones[0:1, :], dst_f[0:1, 0:half], start=True, stop=True)
            mm(bank[1][0:P, 0:TILES - half], ones[0:1, :], dst_f[0:1, half:TILES], start=True, stop=True)
            mm(bank[2][0:SLOTS, 0:CHUNKS], slot_matrix, first_f, start=True, stop=True).then_inc(bases_ready, 1)
            pe.wait_ge(flags_sum, 1)
            mm(bank[3][0:1, 0:1], stat[:, 0, :], ones[:, 0:1], start=True, stop=True).then_inc(flags_sum, 1)
            pe.wait_ge(flag_ready, 1)
            general = pe.value_load(flag_i[0:1, 0:1], min_val=0, max_val=1)
            pe.wait_ge(onehot_ready, 1)
            pe.wait_ge(ones_set, 1)
            pe.wait_ge(w1_in_place, 16 * 2 * MLP_T)

            def edge_mlp(c, s, r, n):
                pe.wait_ge(edges_in[r], n * 16)
                if later(c, 2):
                    pe.wait_ge(hidden_ready, c - 1)
                for h, tiles in enumerate((MLP_T, CH - MLP_T)):
                    rows, at = 1 + tiles * EDGE_FEAT, h * MLP_T * HIDDEN
                    last = mm(mlp_bank[s][0:P, at:at + tiles * HIDDEN], edges_sb[r][0:rows, h * P:(h + 1) * P],
                              w1_blocks[0:rows, 0:tiles * HIDDEN], start=True, stop=True)
                last.then_inc(mlp_done, 1)

            def pick(ph, c, s):
                pe.wait_ge(key_hot_ready, c + (1 + (ph - GCN1) * CHUNKS))
                if later(c, 1):
                    pe.wait_ge(picked_low, c + (ph - GCN1) * CHUNKS)
                for j in range(CH - POOL_T[ph]):
                    to = pick_bank[j // 2][:, (j % 2) * LOWS * FEAT:(j % 2 + 1) * LOWS * FEAT]
                    for a in range(KEYS):
                        for k in range(3):
                            last = mm(to, key_hot[s][:, a * EC + j * P:a * EC + j * P + 128], parts[:, k, a * LOWS * FEAT:(a + 1) * LOWS * FEAT],
                                      start=(a == 0 and k == 0), stop=(a == KEYS - 1 and k == 2))
                last.then_inc(pick_done, 1)

            def window_sums(ph, c, s, r, n):
                if later(c, 2):
                    pe.wait_ge(xsum_copied, c + (ph * CHUNKS - 1))
                if ph == DEG:
                    mm(sum_bank[s][0:FEAT, CW:CW + SLOTS], ones_half[:, :], onehot[:, ds(c * CH, CH), :],
                       start=True, stop=True).then_inc(summed, 1)
                    return
                pe.wait_ge(gathered[ph][r], n * (16 * POOL_T[ph]))
                pe.wait_ge(window_copied, c + (1 + (ph - GCN1) * CHUNKS))
                pe.wait_ge(xsrc_ready, c + (1 + (ph - GCN1) * CHUNKS))
                if ph >= GRU1:
                    pe.wait_ge(xwin_ready, c + (1 + (ph - GRU1) * CHUNKS))
                    pe.wait_ge(hidden_copied, c + (1 + (ph - GRU1) * CHUNKS))
                for j in range(CH):
                    if ph >= GRU1:
                        win = xwin[s][:, j * 128:(j + 1) * 128].rearrange("p (n i) -> p n i", i=FEAT)
                        for q in range(4):
                            mm(sum_bank[s][q * 32:(q + 1) * 32, j * 32:(j + 1) * 32],
                               hidden_ring[s][:, j * HIDDEN:(j + 1) * HIDDEN], win[:, :, q * 4:(q + 1) * 4],
                               start=True, stop=True, tile_position=(0, 32 * q))
                    last = mm(sum_bank[s][0:FEAT, CW + j * WIN:CW + (j + 1) * WIN], xsrc[r][:, j, :],
                              window[s][:, j * WIN:(j + 1) * WIN], start=True, stop=True)
                last.then_inc(summed, 1)

            def slot_sums(ph, c, s):
                pe.wait_ge(xsum_copied, c + (1 + ph * CHUNKS))
                if later(c, 1):
                    pe.wait_ge(slots_copied, c + ph * CHUNKS)
                to = slot_bank[0:SLOTS, 0:FEAT]
                if ph >= GRU1:
                    part = sums_sb[s][:, :].rearrange("p (m r) -> p r m", r=4)
                    for r in range(4):
                        mm(to, part[:, r, :], w2q[:, r, :], start=(r == 0), stop=False)
                    mm(to, xsum_sb[s][:, :], b2m[:, :], start=False, stop=True).then_inc(slotted, 1)
                else:
                    mm(to, xsum_sb[s][:, :], ident[0:FEAT, 0:FEAT], start=True, stop=True).then_inc(slotted, 1)

            def place_slots(ph, c, s):
                pe.wait_ge(slots_copied, c + (1 + ph * CHUNKS))
                pe.wait_ge(place_ready, c + (1 + ph * CHUNKS))
                if later(c, 1):
                    pe.wait_ge(added, c + ph * CHUNKS)
                mm(place_bank[0:FEAT, 0:SPAN], slots_sb[s][:, :], place[s][:, :], start=True, stop=True).then_inc(placed, 1)

            for ph in range(DEG, GRU2 + 1):
                if ph > DEG:
                    pe.wait_ge(table_ready, ph)
                    for t in range(NT):
                        last = mm(bank[t // 4][0:FEAT, (t % 4) * P:(t % 4 + 1) * P], table[:, t, :], ident[:, :],
                                  start=True, stop=True)
                    last.then_inc(table_turned, 1)
                    pe.wait_ge(table_t_ready, ph)
                with pe.If(general < 1):
                    def step(c, s, r, n):
                        if ph > DEG and within(c, 1):
                            pick(ph, c + 1, 1 - s)
                        window_sums(ph, c, s, r, n)
                        if ph == DEG:
                            edge_mlp(c, s, r, n)
                        if later(c, 1):
                            slot_sums(ph, c - 1, 1 - s)
                        if later(c, 2):
                            place_slots(ph, c - 2, s)
                    if ph == GRU1:
                        pe.wait_ge(hidden_ready, CHUNKS)
                    if ph > DEG:
                        pe.wait_ge(parts_ready, ph)
                        pick(ph, 0, 0)
                    steps(pe, step)
                    place_slots(ph, 73, 1)
                    slot_sums(ph, 74, 0)
                    place_slots(ph, 74, 0)
                with pe.Else():
                    if ph == DEG:
                        steps(pe, edge_mlp)
                        pe.wait_ge(hidden_ready, CHUNKS)
                    with pe.Fori(0, TILES) as t:
                        if ph >= GRU1:
                            pe.wait_ge(g_prod_ready, t + (1 + (ph - GRU1) * TILES))
                            pe.wait_ge(g_hidden_copied, t + (1 + (ph - GRU1) * TILES))
                            mm(bank[7][0:HIDDEN, 256:256 + P], g_hidden, ident[:, :],
                               start=True, stop=True).then_inc(g_transposed, 1)
                            pe.wait_ge(g_hidden_ready, t + (1 + (ph - GRU1) * TILES))
                            weights = bank[7][0:P, 0:FEAT * FEAT]
                            mm(weights, g_hidden_t, w2row[:, :], start=True, stop=False)
                            mm(weights, ones[BASE:BASE + 1, :], b2row, start=False, stop=True).then_inc(g_weights, 1)
                            pe.wait_ge(g_msg_ready, t + (1 + (ph - GRU1) * TILES))
                        if ph > DEG:
                            pe.wait_ge(g_gathered[ph], t * 16 + 16)
                        what = ones[:, 0:FEAT] if ph == DEG else g_x[:, :] if ph <= GCN2 else g_msg[:, :]
                        pe.wait_ge(g_wide_ready, t + (1 + ph * TILES))
                        pe.wait_ge(g_added, t + (1 + ph * TILES))
                        for b in range(BLOCKS):
                            last = mm(bank[b][0:FEAT, 0:BLK], what, wide[:, b * BLK:(b + 1) * BLK], start=True, stop=True)
                        last.then_inc(g_blocks, 1)
                pe.nop()
                pe.wait_ge(node_free, ph + 1)
                if ph == DEG:
                    for t in range(NT):
                        last = mm(bank[7][0:P, t * FEAT:(t + 1) * FEAT], acc_view(t), ident[0:FEAT, 0:FEAT], start=True, stop=True)
                    last.then_inc(node_sums, 1)
                elif ph <= GCN2:
                    for t in range(NT):
                        at = slice(t * FEAT, (t + 1) * FEAT)
                        mm(bank[7][0:P, at], acc_view(t), gw[ph - GCN1][:, :], start=True, stop=True)
                        last = mm(bank[6][0:P, at], table_t[:, t * P:(t + 1) * P], gw_self[ph - GCN1], start=True, stop=True)
                    last.then_inc(node_sums, 1)
                else:
                    for t in range(NT):
                        at = slice((t % 10) * GATES, (t % 10 + 1) * GATES)
                        mm(bank[t // 10][0:P, at], acc_view(t), wih[:, :], start=True, stop=True)
                        last = mm(bank[3 + t // 10][0:P, at], table_t[:, t * P:(t + 1) * P], whh, start=True, stop=True)
                    last.then_inc(node_sums, 1)


def kernel(**inputs):
    import numpy as np
    import concourse.bacc as bacc
    from concourse.bass_utils import run_bass_kernel_spmd

    def flat(name, shape):
        return np.ascontiguousarray(np.asarray(inputs[name]).reshape(shape))

    def turned(name, shape):
        return np.ascontiguousarray(np.asarray(inputs[name]).reshape(shape).T)

    slot_matrix = np.concatenate([np.kron(np.eye(CH), np.ones((1, WIN))), np.tile(np.arange(WIN), (1, CH))])
    slot_matrix[0] -= 1
    edge_rows = np.zeros((2 * MLP_T * EDGE_FEAT, CHUNKS, P), np.float32)
    edge_rows[0:CH * EDGE_FEAT] = np.asarray(inputs["edge_attr_13"]).reshape(CHUNKS, CH, P, EDGE_FEAT).transpose(
        1, 3, 0, 2).reshape(CH * EDGE_FEAT, CHUNKS, P)
    arrays = {
        "x": flat("x", (NODES, FEAT)),
        "src": turned("src", (TILES, P)), "src_flat": flat("src", (P, TILES)),
        "keys": np.arange(ROWS * KEYS, dtype=np.float32).reshape(ROWS, KEYS), "dst": turned("dst", (TILES, P)),
        "first": np.ascontiguousarray(np.asarray(inputs["dst"])[::P].reshape(CHUNKS, CH).T),
        "edge_t": np.ascontiguousarray(edge_rows.reshape(2, MLP_T * EDGE_FEAT, CHUNKS, P).transpose(1, 2, 0, 3)).reshape(
            MLP_T * EDGE_FEAT, CHUNKS * 2 * P),
        "w1": flat("L1_gnn_fnet_w1", (EDGE_FEAT, HIDDEN)), "b1": flat("L1_gnn_fnet_b1", (1, HIDDEN)),
        "gw1": flat("L0_gnn_W1", (FEAT, FEAT)), "gb1": flat("L0_gnn_b1", (1, FEAT)),
        "gw2": flat("L0_gnn_W2", (FEAT, FEAT)), "gb2": flat("L0_gnn_b2", (1, FEAT)),
        "w2": flat("L1_gnn_fnet_w2", (HIDDEN, FEAT * FEAT)), "b2": flat("L1_gnn_fnet_b2", (1, FEAT * FEAT)),
        "wih_t": turned("L1_gnn_gru_w_ih", (GATES, FEAT)), "whh_t": turned("L1_gnn_gru_w_hh", (GATES, FEAT)),
        "bih": flat("L1_gnn_gru_b_ih", (1, GATES)), "bhh": flat("L1_gnn_gru_b_hh", (1, GATES)),
        "ident": np.eye(P, dtype=np.float32),
        "iota": np.tile(np.arange(BLK, dtype=np.float32), (P, 1)),
        "slot_matrix": slot_matrix.astype(np.float32),
    }
    nc = bacc.Bacc("TRN2", target_bir_lowering=False, num_devices=1)
    args = [nc.dram_tensor(f"in_{n}", a.shape, mybir.dt.from_np(a.dtype), kind="ExternalInput").ap()
            for n, a in arrays.items()]
    out = nc.dram_tensor("out", (NODES, FEAT), mybir.dt.float32, kind="ExternalOutput").ap()
    gnn_kernel(nc, *args, out)
    r = run_bass_kernel_spmd(nc, [{f"in_{n}": a for n, a in arrays.items()}], core_ids=[0])
    return r.results[0]["out"]
```

```python
import concourse.bass as bass
from concourse import mybir
from contextlib import ExitStack

NODES, FEAT, EDGES, EDGE_FEAT, HIDDEN = 3125, 16, 103125, 13, 32
P = 125
NT = NODES // P
TILES = EDGES // P
CH = 11
CHUNKS = TILES // CH
POOL_T = (None, (4, 5), (4, 5), (5, 6), (5, 6))
PE_MAX = CH - min(min(t) for t in POOL_T[1:])
POOL_MAX = max(max(t) for t in POOL_T[1:])
PAIRS = [0] + [(CH - min(by_parity) + 1) // 2 for by_parity in POOL_T[1:]]
KEYS, LOWS = 2, 13
HELD = KEYS * LOWS
ROWS = -(-NODES // HELD)
EC = PE_MAX * P + PE_MAX % 2
WIN = 8
SLOTS = CH * WIN
SPAN = 64
BLK = 456
BLOCKS = 7
ACCW = BLK * BLOCKS
BASE, TURN = 32, 64
GATES = 3 * FEAT
CW = CH * HIDDEN
XW = CH * WIN * FEAT
QUADS = 17
MLP_T = 6
MLP_ROWS = 1 + MLP_T * EDGE_FEAT
DEG, GCN1, GCN2, GRU1, GRU2 = range(5)


def gnn_kernel(nc, x_in, src_in, src_flat, keys_in, dst_in, first_in, edge_t, w1_in, b1_in, gw1_in, gb1_in, gw2_in, gb2_in,
               w2_in, b2_in, wih_t, whh_t, bih_in, bhh_in, ident_in, iota_in, slot_in, out):
    f32, i32, bf16, f16 = mybir.dt.float32, mybir.dt.int32, mybir.dt.bfloat16, mybir.dt.float16
    ALU, ACT, AX = mybir.AluOpType, mybir.ActivationFunctionType, mybir.AxisListType
    ds = bass.ds
    ctx = ExitStack()
    with ctx:
        def sb(name, shape, dt=f32):
            return ctx.enter_context(nc.sbuf_tensor(name, shape, dt))

        def sem(name):
            return ctx.enter_context(nc.semaphore(name))

        src_i = sb("src_i", [P, TILES], i32)
        onehot = sb("onehot", [P, TILES, WIN], bf16)
        hidden = sb("hidden", [P, TILES * HIDDEN])
        slot_node = sb("slot_node", [SLOTS, CHUNKS])
        ident = sb("ident", [P, P])
        iota = sb("iota", [P, SPAN])
        ones = sb("ones", [P, P])
        ones_half = sb("ones_half", [P, FEAT], bf16)
        w2q = sb("w2q", [128, 4, FEAT])
        b2m = sb("b2m", [FEAT, FEAT])
        gw = [sb("gw1", [FEAT, FEAT]), sb("gw2", [FEAT, FEAT])]
        gb = [sb("gb1", [P, FEAT]), sb("gb2", [P, FEAT])]
        wih = sb("wih", [FEAT, GATES])
        whh = sb("whh", [TURN + FEAT, GATES])[TURN:TURN + FEAT, :]
        bih = sb("bih", [P, GATES])
        bhh = sb("bhh", [P, GATES])
        keys = sb("keys", [ROWS, KEYS])
        low_hot = sb("low_hot", [P, CHUNKS * PE_MAX, LOWS], bf16)
        idx = [sb(f"idx{s}", [P, POOL_MAX], i32) for s in range(4)]
        xsrc = [sb(f"xsrc{s}", [P, CH, FEAT]) for s in range(4)]
        key_row = [sb(f"key_row{s}", [ROWS, EC], f16) for s in range(4)]
        key_hot_full = [sb(f"key_hot{s}", [P, KEYS * EC + 4], bf16) for s in range(2)]
        key_hot = [full[0:ROWS, :] for full in key_hot_full]
        window = [sb(f"window{s}", [P, SLOTS]) for s in range(2)]
        hidden_ring = [sb(f"hidden_ring{s}", [P, CW]) for s in range(2)]
        sums_sb = [sb(f"sums_sb{s}", [128, CW]) for s in range(2)]
        xsum_sb = [sb(f"xsum_sb{s}", [FEAT, SLOTS]) for s in range(2)]
        dst_f = key_hot_full[0][:, 0:2 * TILES].bitcast(f32)
        block_iota = key_hot_full[1][:, 0:2 * BLK].bitcast(f32)
        w2row = sums_sb[0][0:HIDDEN, 0:FEAT * FEAT]
        slots_sb = [sb(f"slots_sb{s}", [SLOTS, FEAT]) for s in range(2)]
        place = [sb(f"place{s}", [SLOTS, SPAN]) for s in range(2)]
        first_i, first_f, slot_matrix = (hidden[0:CH + 1, (7 + k) * TILES:(7 + k) * TILES + w]
                                         for k, w in enumerate((CHUNKS, CHUNKS, SLOTS)))
        first_i = first_i[0:CH, :].bitcast(i32)
        dst_i = hidden[:, 6 * TILES:7 * TILES].bitcast(i32)
        key_f, key_p = (hidden[:, k * TILES:(k + 1) * TILES] for k in (3, 4))
        key_f16 = hidden[:, 5 * TILES:6 * TILES].bitcast(f16)[:, 0:TILES]
        w1_blocks = key_row[3][0:MLP_ROWS, 0:2 * MLP_T * HIDDEN].bitcast(f32)
        scratch = sb("scratch", [P, 3 * NT * GATES])
        edges_sb = [scratch[0:MLP_ROWS, r * 2 * P:(r + 1) * 2 * P] for r in range(4)]
        xwin = [scratch[:, s * XW:(s + 1) * XW] for s in range(2)]
        wide = scratch[:, 0:ACCW]
        gate_i, gate_h, gate_n = (scratch[:, k * NT * GATES:(k + 1) * NT * GATES]
                                  .rearrange("p (t g) -> p t g", g=GATES) for k in range(3))
        rows = sb("rows", [TURN + FEAT, ACCW])
        acc = rows[0:FEAT, :]
        table_t = rows[TURN:TURN + FEAT, 0:NODES]
        first_dst = rows[BASE:BASE + 1, 0:TILES].bitcast(i32)
        b2row = rows[BASE:BASE + 1, TILES:TILES + FEAT * FEAT]
        x0 = sb("x0", [P, NT, FEAT])
        x1 = sb("x1", [P, NT, FEAT])
        table = sb("table", [P, NT, FEAT])
        parts = sb("parts", [ROWS, 3, HELD * FEAT], bf16)
        picked = sb("picked", [P, PE_MAX * LOWS, FEAT])
        held, left = (picked[0:ROWS, k * HELD:(k + 1) * HELD, :].rearrange("p t f -> p (t f)") for k in range(2))
        low_f = picked[:, :, :].rearrange("p t f -> p (t f)")[:, 0:TILES]
        y = sb("y", [P, NT, FEAT])
        z = picked[:, 2 * HELD:2 * HELD + NT, :]
        dinv = sb("dinv", [P, NT, 1])
        inv_deg = sb("inv_deg", [P, NT, 1])
        stat = sb("stat", [P, NT, 1])
        var = sb("var", [P, NT, 1])
        worst = sb("worst", [P, 4])
        flag_f = sb("flag_f", [1, 1])
        flag_i = sb("flag_i", [1, 1], i32)
        g_idx = sb("g_idx", [P, 1], i32)
        g_x = sb("g_x", [P, FEAT])
        g_hidden = hidden_ring[1][:, 0:HIDDEN]
        g_hidden_t = hidden_ring[0][0:HIDDEN, 0:P]
        g_prod = picked[:, 0:FEAT, :]
        g_msg = sb("g_msg", [P, FEAT])

        bank = [ctx.enter_context(nc.psum_tensor(f"bank{i}", [128, 512], f32)) for i in range(8)]
        sum_bank, slot_bank, place_bank, pick_bank, mlp_bank = bank[0:2], bank[2], bank[3], bank[4:8], bank[6:8]

        tables = [None] + [nc.dram_tensor(f"table_dram{k}", [NODES, FEAT], f32).ap() for k in range(1, 5)]
        keys_dram = nc.dram_tensor("keys_dram", [P, TILES], f16).ap()
        keys_flat = keys_dram.rearrange("(o p) t -> o (p t)", o=1)

        ints_in = sem("ints_in")
        consts_in = sem("consts_in")
        edges_in = [sem(f"edges_in{r}") for r in range(4)]
        w1_zero = sem("w1_zero")
        w1_in_place = sem("w1_in_place")
        dst_ready = sem("dst_ready")
        bases_ready = sem("bases_ready")
        flags_sum = sem("flags_sum")
        flag_ready = sem("flag_ready")
        v_step = sem("v_step")
        onehot_ready = sem("onehot_ready")
        idx_ready = sem("idx_ready")
        gather_turn = sem("gather_turn")
        load_turn = sem("load_turn")
        gathered = [None] + [[sem(f"gathered{k}_{s}") for s in range(4)] for k in range(1, 5)]
        ones_set = sem("ones_set")
        keys_made = sem("keys_made")
        keys_stored = sem("keys_stored")
        key_row_in = [sem(f"key_row_in{s}") for s in range(4)]
        low_hot_ready = sem("low_hot_ready")
        key_hot_cleared = sem("key_hot_cleared")
        key_hot_ready = sem("key_hot_ready")
        held_in = sem("held_in")
        parts_ready = sem("parts_ready")
        pick_done = sem("pick_done")
        picked_low = sem("picked_low")
        xsrc_ready = sem("xsrc_ready")
        xwin_ready = sem("xwin_ready")
        place_ready = sem("place_ready")
        summed = sem("summed")
        window_copied = sem("window_copied")
        xsum_copied = sem("xsum_copied")
        slotted = sem("slotted")
        slots_copied = sem("slots_copied")
        placed = sem("placed")
        added = sem("added")
        mlp_done = sem("mlp_done")
        hidden_ready = sem("hidden_ready")
        hidden_copied = sem("hidden_copied")
        g_idx_ready = sem("g_idx_ready")
        g_gathered = [None] + [sem(f"g_gathered{k}") for k in range(1, 5)]
        g_hidden_copied = sem("g_hidden_copied")
        g_transposed = sem("g_transposed")
        g_hidden_ready = sem("g_hidden_ready")
        g_weights_begun = sem("g_weights_begun")
        g_weights = sem("g_weights")
        g_prod_ready = sem("g_prod_ready")
        g_msg_ready = sem("g_msg_ready")
        g_wide_ready = sem("g_wide_ready")
        g_blocks = sem("g_blocks")
        g_added = sem("g_added")
        table_ready = sem("table_ready")
        table_stored = sem("table_stored")
        table_turned = sem("table_turned")
        table_t_ready = sem("table_t_ready")
        node_sums = sem("node_sums")
        node_hidden = sem("node_hidden")
        node_free = sem("node_free")
        rz_in = sem("rz_in")
        rz_out = sem("rz_out")
        n_in = sem("n_in")
        n_out = sem("n_out")
        sqrt_in = sem("sqrt_in")
        sqrt_out = sem("sqrt_out")
        out_ready = sem("out_ready")
        out_stored = sem("out_stored")

        N_CONSTS = 20
        SLOT_USES = [len(range(r, CHUNKS, 4)) for r in range(4)]
        ROOTS = (DEG, GCN2, GRU2)

        def steps(eng, step):
            for c in range(4):
                step(c, c % 2, c % 4, c // 4 + 1)
            with nc.Fori(0, QUADS, engines=[eng.engine], hint_back_edge=True) as i:
                for k in range(4, 8):
                    step(i * 4 + k, k % 2, k % 4, i + (k // 4 + 1))
            for c in (72, 73, 74):
                step(c, c % 2, c % 4, c // 4 + 1)

        def pairs_until(ph, c):
            return c * PAIRS[ph] + CHUNKS * sum(PAIRS[:ph])

        def pair_count(ph, s, j):
            own = (CH - POOL_T[ph][s] + 1) // 2
            return 1 if j // 2 < own - 1 else 1 + PAIRS[ph] - own

        def later(c, n):
            return not isinstance(c, int) or c >= n

        def within(c, ahead):
            return not isinstance(c, int) or c + ahead < CHUNKS

        acc_turned = acc[:, 0:NODES].rearrange("f (p t) -> f t p", t=NT)

        def acc_view(t):
            return acc_turned[:, t, :]

        HIDDEN_AT = ((7, 0, 0, 10), (2, 16, 10, 20), (3, 64, 20, NT))
        INPUT_AT = ((0, 0, 0, 10), (1, 0, 10, 20), (4, 0, 20, NT))

        block = ctx.enter_context(nc.Block())

        @block.sync
        def _(sp):
            sp.dma_start(dst_i, dst_in).then_inc(ints_in, 16)
            sp.dma_start(first_i, first_in).then_inc(ints_in, 16)
            sp.dma_start(first_dst, dst_in[0:1, :]).then_inc(ints_in, 16)
            sp.dma_start(src_i[:, :], src_in).then_inc(ints_in, 16)
            sp.dma_start(low_f.bitcast(i32), src_flat).then_inc(ints_in, 16)
            loads = [(ident[:, :], ident_in), (iota[:, :], iota_in[:, 0:SPAN]), (block_iota, iota_in), (keys[:, :], keys_in), (slot_matrix, slot_in),
                     (x0[:, :, :], x_in.rearrange("(p t) f -> p t f", t=NT)),
                     (b2m[:, :], b2_in.rearrange("a (i o) -> (a i) o", o=FEAT)), (b2row, b2_in),
                     (w2row, w2_in), (gw[0][:, :], gw1_in), (gw[1][:, :], gw2_in),
                     (wih[:, :], wih_t), (whh, whh_t)]
            loads += [(w2q[q * HIDDEN:(q + 1) * HIDDEN, :, :],
                       w2_in[:, q * 64:(q + 1) * 64].rearrange("k (i o) -> k i o", o=FEAT)) for q in range(4)]
            loads += [(gb[0][:, :], gb1_in.to_broadcast([P, FEAT])), (gb[1][:, :], gb2_in.to_broadcast([P, FEAT])),
                      (bih[:, :], bih_in.to_broadcast([P, GATES])), (bhh[:, :], bhh_in.to_broadcast([P, GATES]))]
            assert len(loads) == N_CONSTS + 1
            for to, what in loads:
                sp.dma_start(to, what).then_inc(consts_in, 16)

            sp.wait_ge(w1_zero, 1)
            for j in range(MLP_T):
                at = slice(j * HIDDEN, (j + 1) * HIDDEN)
                sp.dma_start(w1_blocks[1 + j * EDGE_FEAT:1 + (j + 1) * EDGE_FEAT, at], w1_in).then_inc(w1_in_place, 16)
                sp.dma_start(w1_blocks[0:1, at], b1_in).then_inc(w1_in_place, 16)
            sp.wait_ge(keys_made, 1)
            sp.dma_start(keys_dram, key_f16).then_inc(keys_stored, 16)
            sp.wait_ge(keys_stored, 16)

            def load_keys(ph, c, r):
                if later(c, 4):
                    sp.wait_ge(key_hot_ready, c + ((ph - GCN1) * CHUNKS - 3))
                    sp.sem_inc(load_turn, 1)
                w = (CH - POOL_T[ph][r % 2]) * P
                sp.dma_start(key_row[r][:, 0:w], keys_flat[:, ds(c * (CH * P) + POOL_T[ph][r % 2] * P, w)].to_broadcast([ROWS, w])
                             ).then_inc(key_row_in[r], 16)

            def load_edges(c, s, r, n):
                if later(c, 4):
                    sp.wait_ge(mlp_done, c - 3)
                    sp.sem_inc(load_turn, 1)
                sp.dma_start(edges_sb[r][1:MLP_ROWS, :], edge_t[:, ds(c * (2 * P), 2 * P)]).then_inc(edges_in[r], 16)

            sp.wait_ge(flag_ready, 1)
            general = sp.value_load(flag_i[0:1, 0:1], min_val=0, max_val=1)
            steps(sp, load_edges)
            with sp.If(general < 1):
                load_keys(GCN1, 0, 0)
                load_keys(GCN1, 1, 1)
            sp.nop()
            for k in range(1, 5):
                sp.wait_ge(table_ready, k)
                sp.dma_start(tables[k].rearrange("(p t) f -> p t f", t=NT), table[:, :, :]).then_inc(table_stored, 16)
                sp.wait_ge(table_stored, 16 * k)
                whole = ROWS - 1
                sp.dma_start(held[0:whole, :], tables[k][0:whole * HELD, :].rearrange("(p t) f -> p (t f)", t=HELD)
                             ).then_inc(held_in, 16)
                rest = (NODES - whole * HELD) * FEAT
                sp.dma_start(held[whole:ROWS, 0:rest], tables[k][whole * HELD:NODES, :].rearrange("(o t) f -> o (t f)", o=1)
                             ).then_inc(held_in, 16)

                def step(c, s, r, n):
                    if within(c, 2):
                        load_keys(k, c + 2, (r + 2) % 4)

                with sp.If(general < 1):
                    steps(sp, step)
                    if k < GRU2:
                        for c in range(2):
                            sp.wait_ge(key_hot_ready, (k - GCN1) * CHUNKS + (73 + c))
                            load_keys(k + 1, c, c)
                sp.nop()
            sp.wait_ge(table_stored, 64)
            sp.wait_ge(out_ready, 1)
            sp.dma_start(out.rearrange("(p t) f -> p t f", t=NT), y[:, :, :]).then_inc(out_stored, 16)
            sp.wait_ge(out_stored, 16)

        @block.gpsimd
        def _(pool):
            pool.wait_ge(flag_ready, 1)
            general = pool.value_load(flag_i[0:1, 0:1], min_val=0, max_val=1)
            for ph in range(GCN1, GRU2 + 1):
                pool.wait_ge(table_stored, 16 * ph)
                with pool.If(general < 1):
                    def gather(c, s, r, n):
                        pool.wait_ge(idx_ready, c + (1 + (ph - 1) * CHUNKS))
                        if later(c, 4):
                            pool.wait_ge(summed, c + (ph * CHUNKS - 3))
                        pool.sem_inc(gather_turn, 1)
                        for j in range(POOL_T[ph][s]):
                            pool.indirect_dma_start(
                                out=xsrc[r][:, j, :], out_offset=None, in_=tables[ph],
                                in_offset=bass.IndirectOffsetOnAxis(ap=idx[r][:, j:j + 1], axis=0)
                            ).then_inc(gathered[ph][r], 16)
                    steps(pool, gather)
                with pool.Else():
                    with pool.Fori(0, TILES) as t:
                        pool.wait_ge(g_idx_ready, t + (1 + (ph - 1) * TILES))
                        pool.sem_inc(gather_turn, 1)
                        pool.indirect_dma_start(
                            out=g_x[:, :], out_offset=None, in_=tables[ph],
                            in_offset=bass.IndirectOffsetOnAxis(ap=g_idx[:, 0:1], axis=0)
                        ).then_inc(g_gathered[ph], 16)
                pool.nop()

        @block.scalar
        def _(act):
            act.wait_ge(flag_ready, 1)
            act.wait_ge(onehot_ready, 1)
            act.wait_ge(keys_stored, 16)
            general = act.value_load(flag_i[0:1, 0:1], min_val=0, max_val=1)

            def relu_hidden(c, s, r, n):
                act.wait_ge(mlp_done, c + 1)
                nc.scalar.activation(hidden[:, ds(c * CW, CW)], mlp_bank[s][0:P, 0:CW], ACT.Relu).then_inc(hidden_ready, 1)

            def copy_hidden(ph, c, s):
                if later(c, 2):
                    act.wait_ge(summed, c + (ph * CHUNKS - 1))
                nc.scalar.activation(hidden_ring[s][:, :], hidden[:, ds(c * CW, CW)], ACT.Copy).then_inc(hidden_copied, 1)

            def copy_window(ph, c, s):
                if later(c, 2):
                    act.wait_ge(summed, c + (ph * CHUNKS - 1))
                nc.scalar.activation(window[s][:, :].rearrange("p (j n) -> p j n", n=WIN), onehot[:, ds(c * CH, CH), :], ACT.Copy
                                     ).then_inc(window_copied, 1)

            def copy_sums(ph, c, s):
                act.wait_ge(summed, c + (1 + ph * CHUNKS))
                if later(c, 2):
                    act.wait_ge(slotted, c + (ph * CHUNKS - 1))
                if ph >= GRU1:
                    nc.scalar.activation(sums_sb[s][:, :], sum_bank[s][:, 0:CW], ACT.Copy)
                nc.scalar.activation(xsum_sb[s][:, :], sum_bank[s][0:FEAT, CW:CW + SLOTS], ACT.Copy).then_inc(xsum_copied, 1)

            def copy_slots(ph, c, s):
                act.wait_ge(slotted, c + (1 + ph * CHUNKS))
                if later(c, 2):
                    act.wait_ge(placed, c + (ph * CHUNKS - 1))
                nc.scalar.activation(slots_sb[s][:, :], slot_bank[0:SLOTS, 0:FEAT], ACT.Copy).then_inc(slots_copied, 1)

            for ph in range(DEG, GRU2 + 1):
                if ph == GRU1:
                    act.wait_ge(hidden_ready, CHUNKS)
                if ph > DEG:
                    for k, banks in enumerate((range(4, 7), range(4))):
                        act.wait_ge(table_turned, 2 * ph - 1 + k)
                        for b in banks:
                            t0, t1 = 4 * b, min(4 * b + 4, NT)
                            if ph <= GCN2:
                                last = nc.scalar.activation(acc_turned[:, t0:t1, :],
                                                            bank[b][0:FEAT, 0:(t1 - t0) * P].rearrange("f (t p) -> f t p", p=P), ACT.Copy)
                            else:
                                last = nc.scalar.activation(table_t[:, t0 * P:t1 * P], bank[b][0:FEAT, 0:(t1 - t0) * P], ACT.Copy)
                        last.then_inc(table_t_ready, 1)
                with act.If(general < 1):
                    def step(c, s, r, n):
                        if ph > DEG:
                            copy_window(ph, c, s)
                        if ph >= GRU1:
                            copy_hidden(ph, c, s)
                        copy_sums(ph, c, s)
                        if ph == DEG:
                            relu_hidden(c, s, r, n)
                        if later(c, 1):
                            copy_slots(ph, c - 1, 1 - s)
                    steps(act, step)
                    copy_slots(ph, CHUNKS - 1, 0)
                with act.Else():
                    if ph == DEG:
                        steps(act, relu_hidden)
                    if ph >= GRU1:
                        with act.Fori(0, TILES) as t:
                            act.wait_ge(g_transposed, t + (2 + (ph - GRU1) * TILES))
                            nc.scalar.activation(g_hidden_t, bank[7][0:HIDDEN, 256:256 + P], ACT.Copy).then_inc(g_hidden_ready, 1)
                act.nop()
                if ph >= GRU1:
                    act.wait_ge(rz_in, ph - GRU1 + 1)
                    nc.scalar.activation(gate_i[:, :, 0:32], gate_i[:, :, 0:32], ACT.Sigmoid).then_inc(rz_out, 1)
                    act.wait_ge(n_in, ph - GRU1 + 1)
                    nc.scalar.activation(gate_n[:, :, 0:16], gate_n[:, :, 0:16], ACT.Tanh).then_inc(n_out, 1)
                if ph in ROOTS:
                    act.wait_ge(sqrt_in, ROOTS.index(ph) + 1)
                    nc.scalar.activation(var[:, :, :], var[:, :, :], ACT.Sqrt).then_inc(sqrt_out, 1)

        @block.vector
        def _(dve):
            chained = [0]

            def link(ins):
                chained[0] += 1
                ins.then_inc(v_step, 1)
                dve.wait_ge(v_step, chained[0])

            for free in (g_blocks, g_added, g_transposed, g_prod_ready):
                dve.sem_inc(free, 1)
            nc.vector.memset(ones[:, :], 1.0)
            nc.vector.memset(ones_half[:, :], 1.0)
            nc.vector.memset(w1_blocks, 0.0).then_inc(w1_zero, 1)
            nc.vector.memset(scratch[0:1, 0:4 * 2 * P], 1.0).then_inc(ones_set, 1)
            nc.vector.memset(acc[:, :], 0.0)
            link(nc.vector.memset(first_f, 1.0))
            dve.wait_ge(ints_in, 80)
            nc.vector.tensor_copy(first_f[0:CH, :], first_i)
            nc.vector.tensor_copy(dst_f, dst_i).then_inc(dst_ready, 1)
            dve.wait_ge(dst_ready, 1)
            for src, twice in ((low_f.bitcast(i32), key_f), (src_i[:, :], key_p)):
                link(nc.vector.tensor_copy(twice, src))
                link(nc.vector.tensor_scalar(twice, twice, -float(LOWS // 2), 1.0 / LOWS, ALU.add, ALU.mult))
                link(nc.vector.tensor_scalar(twice, twice, 12582912.0, None, ALU.add))
                link(nc.vector.tensor_scalar(twice, twice, -12582912.0, None, ALU.add))
            nc.vector.tensor_copy(key_f16, key_f).then_inc(keys_made, 1)
            link(nc.vector.tensor_copy(low_f, src_i[:, :]))
            link(nc.vector.scalar_tensor_tensor(low_f, key_p, -float(LOWS), low_f, ALU.mult, ALU.add))
            dve.wait_ge(consts_in, 16 * (N_CONSTS + 1))
            dve.wait_ge(bases_ready, 1)
            half = 35 * CH
            rel = hidden[:, 0:TILES]
            from_chunk = hidden[:, TILES:2 * TILES]
            for n0, n1, b in ((0, half, 0), (half, TILES, 1)):
                base = bank[b][0:P, 0:n1 - n0]
                nc.vector.tensor_tensor(rel[:, n0:n1], dst_f[:, n0:n1], base, ALU.subtract)
                chunk_base = base.rearrange("p (c j) -> p c j", j=CH)[:, :, 0:1].to_broadcast([P, (n1 - n0) // CH, CH])
                last = nc.vector.tensor_tensor(from_chunk[:, n0:n1].rearrange("p (c j) -> p c j", j=CH),
                                               dst_f[:, n0:n1].rearrange("p (c j) -> p c j", j=CH), chunk_base, ALU.subtract)
            link(last)
            nc.vector.tensor_copy(slot_node[:, :], bank[2][0:SLOTS, 0:CHUNKS])
            nc.vector.tensor_tensor(onehot[:, :, :], rel.rearrange("p (t o) -> p t o", o=1).to_broadcast([P, TILES, WIN]),
                                    iota[:, 0:WIN].rearrange("p (o w) -> p o w", o=1).to_broadcast([P, TILES, WIN]),
                                    ALU.is_equal).then_inc(onehot_ready, 1)
            nc.vector.tensor_reduce(worst[:, 0:1], rel, AX.X, ALU.max)
            nc.vector.tensor_reduce(worst[:, 1:2], from_chunk, AX.X, ALU.max)
            nc.vector.tensor_reduce(worst[:, 2:3], rel, AX.X, ALU.min)
            link(nc.vector.tensor_reduce(worst[:, 3:4], from_chunk, AX.X, ALU.min))
            nc.vector.tensor_scalar(worst[:, 0:1], worst[:, 0:1], float(WIN), None, ALU.is_ge)
            nc.vector.tensor_scalar(worst[:, 1:2], worst[:, 1:2], float(SPAN), None, ALU.is_ge)
            link(nc.vector.tensor_scalar(worst[:, 2:4], worst[:, 2:4], 0.0, None, ALU.is_lt))
            link(nc.vector.tensor_reduce(var[:, 0, :], worst[:, :], AX.X, ALU.max))
            nc.vector.tensor_copy(stat[:, 0, :], var[:, 0, :]).then_inc(flags_sum, 1)
            dve.wait_ge(flags_sum, 2)
            link(nc.vector.tensor_scalar(flag_f[:, :], bank[3][0:1, 0:1], 0.5, None, ALU.is_ge))
            link(nc.vector.tensor_copy(flag_i[:, :], flag_f[:, :]))
            dve.nop().then_inc(flag_ready, 1)
            general = dve.value_load(flag_i[0:1, 0:1], min_val=0, max_val=1)

            def window_first(c):
                return dve.value_load(first_dst[0:1, ds(c * CH, 1)], min_val=0, max_val=NODES - 1)

            def add_placed(ph, c, s, first):
                dve.wait_ge(placed, c + (1 + ph * CHUNKS))
                if later(c, 1):
                    dve.wait_ge(added, c + ph * CHUNKS)
                nodes = acc[:, ds(first, SPAN)]
                nc.vector.tensor_tensor(nodes, nodes, place_bank[0:FEAT, 0:SPAN], ALU.add).then_inc(added, 1)

            def take_idx(ph, c, r, n):
                if later(c, 4):
                    dve.wait_ge(gathered[ph][r], (n - 1) * (16 * POOL_T[ph][r % 2]))
                nc.vector.tensor_copy(idx[r][:, 0:POOL_T[ph][r % 2]], src_i[:, ds(c * CH, POOL_T[ph][r % 2])]).then_inc(idx_ready, 1)

            def make_key_hot(ph, c, s, r, n):
                dve.wait_ge(key_row_in[r], (n + (ph - GCN1) * SLOT_USES[r]) * 16)
                if later(c, 2):
                    dve.wait_ge(pick_done, pairs_until(ph, c) - PAIRS[ph])
                w = (CH - POOL_T[ph][s]) * P
                for a in range(KEYS):
                    last = nc.vector.tensor_scalar(key_hot[s][:, a * EC:a * EC + w], key_row[r][:, 0:w], keys[:, a:a + 1], None, ALU.is_equal)
                last.then_inc(key_hot_ready, 1)

            def pick_low(ph, c, s, r):
                if later(c, 4):
                    dve.wait_ge(summed, c + (ph * CHUNKS - 3))
                if later(c, 1):
                    dve.wait_ge(xsrc_ready, c + (ph - GCN1) * CHUNKS)
                mine = CH - POOL_T[ph][s]
                for j in range(0, mine, 2):
                    m = min(2, mine - j) * LOWS
                    dve.wait_ge(pick_done, pairs_until(ph, c) + (j // 2 + 1))
                    low = low_hot[:, ds(c * PE_MAX + (PE_MAX - mine + j), m // LOWS), :]
                    nc.vector.tensor_tensor(
                        picked[:, j * LOWS:j * LOWS + m, :], pick_bank[j // 2][0:P, 0:m * FEAT].rearrange("p (m f) -> p m f", f=FEAT),
                        low.rearrange("p j (b o) -> p (j b) o", o=1).to_broadcast([P, m, FEAT]), ALU.mult).then_inc(picked_low, pair_count(ph, s, j))
                dve.wait_ge(picked_low, pairs_until(ph, c) + PAIRS[ph])
                nc.vector.tensor_reduce(xsrc[r][:, POOL_T[ph][s]:CH, :],
                                        picked[:, 0:mine * LOWS, :].rearrange("p (j b) f -> p j f b", b=LOWS),
                                        AX.X, ALU.add).then_inc(xsrc_ready, 1)

            def split_table(ph):
                dve.wait_ge(held_in, 32 * ph)
                link(nc.vector.tensor_copy(parts[:, 0, :], held))
                link(nc.vector.tensor_tensor(left, held, parts[:, 0, :], ALU.subtract))
                link(nc.vector.tensor_copy(parts[:, 1, :], left))
                link(nc.vector.tensor_tensor(left, left, parts[:, 1, :], ALU.subtract))
                nc.vector.tensor_copy(parts[:, 2, :], left).then_inc(parts_ready, 1)

            def make_place(ph, c, s):
                if later(c, 2):
                    dve.wait_ge(placed, c + (ph * CHUNKS - 1))
                nc.vector.tensor_scalar(place[s][:, :], iota[0:SLOTS, 0:SPAN], slot_node[:, ds(c, 1)], None,
                                        ALU.is_equal).then_inc(place_ready, 1)

            def widen(ph, c, s, r, n):
                dve.wait_ge(gathered[ph][r], n * (16 * POOL_T[ph][s]))
                if ph >= GRU1:
                    dve.wait_ge(xsrc_ready, c + (1 + (ph - GCN1) * CHUNKS))
                    if later(c, 2):
                        dve.wait_ge(summed, c + (ph * CHUNKS - 1))
                    nc.vector.tensor_tensor(
                        xwin[s].rearrange("p (j n i) -> p j n i", n=WIN, i=FEAT),
                        xsrc[r][:, :, :].rearrange("p j (o i) -> p j o i", o=1).to_broadcast([P, CH, WIN, FEAT]),
                        onehot[:, ds(c * CH, CH), :].rearrange("p j (n o) -> p j n o", o=1).to_broadcast([P, CH, WIN, FEAT]),
                        ALU.mult).then_inc(xwin_ready, 1)

            def over_nodes(row, tiles):
                return row.rearrange("p (o g) -> p o g", o=1).to_broadcast([P, tiles, row.shape[1]])

            def normalise(to, turn):
                link(nc.vector.tensor_reduce(stat[:, :, :], y[:, :, :], AX.X, ALU.add))
                link(nc.vector.tensor_scalar(stat[:, :, :], stat[:, :, :], 1.0 / FEAT, None, ALU.mult))
                link(nc.vector.tensor_tensor(y[:, :, :], y[:, :, :], stat[:, :, :].to_broadcast([P, NT, FEAT]), ALU.subtract))
                link(nc.vector.tensor_tensor(z[:, :, :], y[:, :, :], y[:, :, :], ALU.mult))
                link(nc.vector.tensor_reduce(var[:, :, :], z[:, :, :], AX.X, ALU.add))
                nc.vector.tensor_scalar(var[:, :, :], var[:, :, :], 1.0 / FEAT, 1e-5, ALU.mult, ALU.add).then_inc(sqrt_in, 1)
                dve.wait_ge(sqrt_out, turn)
                link(nc.vector.reciprocal(var[:, :, :], var[:, :, :]))
                return nc.vector.tensor_tensor(to, y[:, :, :], var[:, :, :].to_broadcast([P, NT, FEAT]), ALU.mult)

            for ph in range(DEG, GRU2 + 1):
                if ph >= GRU1:
                    link(nc.vector.memset(acc[:, :], 0.0))
                if ph > DEG:
                    split_table(ph)
                with dve.If(general < 1):
                    def step(c, s, r, n):
                        if ph > DEG and within(c, 2):
                            make_key_hot(ph, c + 2, s, (r + 2) % 4, n + (r + 2) // 4)
                        if later(c, 3):
                            add_placed(ph, c - 3, 1 - s, window_first(c - 3))
                        if ph > DEG:
                            if within(c, 3):
                                take_idx(ph, c + 3, (r + 3) % 4, n + (r + 3) // 4)
                            widen(ph, c, s, r, n)
                        if later(c, 1):
                            make_place(ph, c - 1, 1 - s)
                        if ph > DEG and within(c, 1):
                            pick_low(ph, c + 1, 1 - s, (r + 1) % 4)
                    if ph == DEG:
                        for full in key_hot:
                            nc.vector.memset(full, 0.0).then_inc(key_hot_cleared, 1)
                        dve.wait_ge(key_hot_cleared, 2)
                    else:
                        pick_low(ph, 0, 0, 0)
                    steps(dve, step)
                    make_place(ph, 74, 0)
                    for c, first in [(c, window_first(c)) for c in (72, 73, 74)]:
                        add_placed(ph, c, c % 2, first)
                    dve.wait_ge(added, (ph + 1) * CHUNKS)
                    dve.nop().then_inc(node_free, 1)
                    if ph == DEG:
                        lows = low_f.rearrange("p (c j) -> p c j", j=CH)
                        for j in range(PE_MAX):
                            at = low_hot[:, :, :].rearrange("p (c j) w -> p c j w", j=PE_MAX)[:, :, j, :]
                            of = lows[:, :, CH - PE_MAX + j:CH - PE_MAX + j + 1].to_broadcast([P, CHUNKS, LOWS])
                            nc.vector.tensor_tensor(at, of, iota[:, 0:LOWS].rearrange("p (o w) -> p o w", o=1)
                                                    .to_broadcast([P, CHUNKS, LOWS]), ALU.is_equal).then_inc(low_hot_ready, 1)
                        dve.wait_ge(low_hot_ready, PE_MAX)
                    if ph < GRU2:
                        for c in range(3):
                            take_idx(ph + 1, c, c, 1)
                        make_key_hot(ph + 1, 0, 0, 0, 1)
                        make_key_hot(ph + 1, 1, 1, 1, 1)
                with dve.Else():
                    if ph == DEG:
                        dve.wait_ge(mlp_done, CHUNKS)
                    with dve.Fori(0, TILES) as t:
                        if ph > DEG:
                            dve.wait_ge(g_blocks, t + (1 + ph * TILES))
                            nc.vector.tensor_copy(g_idx[:, :], src_i[:, ds(t, 1)]).then_inc(g_idx_ready, 1)
                        if ph >= GRU1:
                            dve.wait_ge(g_transposed, t + (1 + (ph - GRU1) * TILES))
                            nc.vector.tensor_copy(g_hidden, hidden[:, ds(t * HIDDEN, HIDDEN)]).then_inc(g_hidden_copied, 1)
                        dve.wait_ge(g_blocks, t + (1 + ph * TILES))
                        for b in range(BLOCKS):
                            last = nc.vector.tensor_scalar(wide[:, b * BLK:(b + 1) * BLK], block_iota, float(b * BLK),
                                                           dst_f[:, ds(t, 1)], ALU.add, ALU.is_equal)
                        last.then_inc(g_wide_ready, 1)
                        if ph > DEG:
                            dve.wait_ge(g_gathered[ph], t * 16 + 16)
                        if ph >= GRU1:
                            dve.wait_ge(g_weights, t + (1 + (ph - GRU1) * TILES))
                            nc.vector.tensor_tensor(g_prod, bank[7][0:P, 0:FEAT * FEAT].rearrange("p (i o) -> p i o", o=FEAT),
                                                    g_x[:, :].rearrange("p (i o) -> p i o", o=1).to_broadcast([P, FEAT, FEAT]),
                                                    ALU.mult).then_inc(g_prod_ready, 1)
                            dve.wait_ge(g_prod_ready, t + (2 + (ph - GRU1) * TILES))
                            nc.vector.tensor_reduce(g_msg[:, :], g_prod.rearrange("p i o -> p o i"), AX.X, ALU.add).then_inc(g_msg_ready, 1)
                        dve.wait_ge(g_blocks, t + (2 + ph * TILES))
                        dve.wait_ge(g_added, t + (1 + ph * TILES))
                        for b in range(BLOCKS):
                            part = acc[:, b * BLK:(b + 1) * BLK]
                            last = nc.vector.tensor_tensor(part, part, bank[b][0:FEAT, 0:BLK], ALU.add)
                        last.then_inc(g_added, 1)
                    dve.wait_ge(g_added, 1 + (ph + 1) * TILES)
                    dve.nop().then_inc(node_free, 1)
                if ph < GRU2:
                    nc.vector.memset(held, 0.0)
                if ph >= GRU1:
                    dve.wait_ge(node_hidden, (ph - GRU1 + 1) * 3)
                    for b, c0, t0, t1 in HIDDEN_AT:
                        w = (t1 - t0) * GATES
                        last = nc.vector.tensor_tensor(gate_h[:, t0:t1, :], bank[b][0:P, c0:c0 + w].rearrange("p (t g) -> p t g", g=GATES),
                                                       over_nodes(bhh[:, :], t1 - t0), ALU.add)
                    link(last)
                    nc.vector.tensor_tensor(gate_h[:, :, 0:32], gate_h[:, :, 0:32], over_nodes(bih[:, 0:32], NT), ALU.add)
                link(dve.nop())
                dve.wait_ge(node_sums, ph + 1)
                if ph == DEG:
                    count = bank[7][0:P, 0:NT * FEAT].rearrange("p (t f) -> p t f", f=FEAT)[:, :, 0:1]
                    nc.vector.tensor_scalar(stat[:, :, :], count, 1.0, None, ALU.max)
                    nc.vector.tensor_scalar(var[:, :, :], count, 1.0, None, ALU.add).then_inc(sqrt_in, 1)
                    dve.wait_ge(sqrt_out, 1)
                    link(nc.vector.reciprocal(dinv[:, :, :], var[:, :, :]))
                    link(nc.vector.reciprocal(inv_deg[:, :, :], stat[:, :, :]))
                    nc.vector.tensor_tensor(table[:, :, :], x0[:, :, :], dinv[:, :, :].to_broadcast([P, NT, FEAT]),
                                            ALU.mult).then_inc(table_ready, 1)
                elif ph <= GCN2:
                    sums = bank[7][0:P, 0:NT * FEAT].rearrange("p (t f) -> p t f", f=FEAT)
                    link(nc.vector.tensor_tensor(y[:, :, :], sums, dinv[:, :, :].to_broadcast([P, NT, FEAT]), ALU.mult))
                    link(nc.vector.tensor_tensor(y[:, :, :], y[:, :, :], over_nodes(gb[ph - GCN1][:, :], NT), ALU.add))
                    dve.wait_ge(table_stored, 16 * ph)
                    dve.wait_ge(table_turned, 2 * ph)
                    if ph == GCN1:
                        link(nc.vector.tensor_scalar(y[:, :, :], y[:, :, :], 0.0, None, ALU.max))
                        nc.vector.tensor_tensor(table[:, :, :], y[:, :, :], dinv[:, :, :].to_broadcast([P, NT, FEAT]),
                                                ALU.mult).then_inc(table_ready, 1)
                    else:
                        link(nc.vector.tensor_tensor(y[:, :, :], y[:, :, :], x0[:, :, :], ALU.add))
                        link(normalise(x1[:, :, :], 2))
                        nc.vector.tensor_copy(table[:, :, :], x1[:, :, :]).then_inc(table_ready, 1)
                else:
                    for b, c0, t0, t1 in INPUT_AT:
                        last = nc.vector.tensor_tensor(gate_i[:, t0:t1, :],
                                                       bank[b][0:P, c0:c0 + (t1 - t0) * GATES].rearrange("p (t g) -> p t g", g=GATES),
                                                       inv_deg[:, t0:t1, :].to_broadcast([P, t1 - t0, GATES]), ALU.mult)
                    link(last)
                    nc.vector.tensor_tensor(gate_i[:, :, 0:32], gate_i[:, :, 0:32], gate_h[:, :, 0:32], ALU.add).then_inc(rz_in, 1)
                    link(nc.vector.tensor_tensor(gate_i[:, :, 32:48], gate_i[:, :, 32:48], over_nodes(bih[:, 32:48], NT), ALU.add))
                    dve.wait_ge(rz_out, ph - GRU1 + 1)
                    link(nc.vector.tensor_tensor(gate_n[:, :, 0:16], gate_i[:, :, 0:16], gate_h[:, :, 32:48], ALU.mult))
                    nc.vector.tensor_tensor(gate_n[:, :, 0:16], gate_n[:, :, 0:16], gate_i[:, :, 32:48], ALU.add).then_inc(n_in, 1)
                    dve.wait_ge(n_out, ph - GRU1 + 1)
                    link(nc.vector.tensor_tensor(y[:, :, :], table[:, :, :], gate_n[:, :, 0:16], ALU.subtract))
                    link(nc.vector.tensor_tensor(y[:, :, :], y[:, :, :], gate_i[:, :, 16:32], ALU.mult))
                    if ph == GRU1:
                        dve.wait_ge(table_stored, 16 * ph)
                        dve.wait_ge(table_turned, 2 * ph)
                        nc.vector.tensor_tensor(table[:, :, :], y[:, :, :], gate_n[:, :, 0:16], ALU.add).then_inc(table_ready, 1)
                    else:
                        link(nc.vector.tensor_tensor(y[:, :, :], y[:, :, :], gate_n[:, :, 0:16], ALU.add))
                        link(nc.vector.tensor_tensor(y[:, :, :], y[:, :, :], x1[:, :, :], ALU.add))
                        link(normalise(z[:, :, :], 3))
                        nc.vector.tensor_copy(y[:, :, :], z[:, :, :]).then_inc(out_ready, 1)

        @block.tensor
        def _(pe):
            mm = nc.tensor.matmul
            pe.wait_ge(dst_ready, 1)
            pe.wait_ge(consts_in, 16 * (N_CONSTS + 1))
            half = 35 * CH
            mm(bank[0][0:P, 0:half], ones[0:1, :], dst_f[0:1, 0:half], start=True, stop=True)
            mm(bank[1][0:P, 0:TILES - half], ones[0:1, :], dst_f[0:1, half:TILES], start=True, stop=True)
            mm(bank[2][0:SLOTS, 0:CHUNKS], slot_matrix, first_f, start=True, stop=True).then_inc(bases_ready, 1)
            pe.wait_ge(flags_sum, 1)
            mm(bank[3][0:1, 0:1], stat[:, 0, :], ones[:, 0:1], start=True, stop=True).then_inc(flags_sum, 1)
            pe.wait_ge(flag_ready, 1)
            general = pe.value_load(flag_i[0:1, 0:1], min_val=0, max_val=1)
            pe.wait_ge(onehot_ready, 1)
            pe.wait_ge(ones_set, 1)
            pe.wait_ge(w1_in_place, 16 * 2 * MLP_T)

            def edge_mlp(c, s, r, n):
                pe.wait_ge(edges_in[r], n * 16)
                if later(c, 2):
                    pe.wait_ge(hidden_ready, c - 1)
                for h, tiles in enumerate((MLP_T, CH - MLP_T)):
                    rows, at = 1 + tiles * EDGE_FEAT, h * MLP_T * HIDDEN
                    last = mm(mlp_bank[s][0:P, at:at + tiles * HIDDEN], edges_sb[r][0:rows, h * P:(h + 1) * P],
                              w1_blocks[0:rows, 0:tiles * HIDDEN], start=True, stop=True)
                last.then_inc(mlp_done, 1)

            def hidden_gates(ph, k):
                b, c0, t0, t1 = HIDDEN_AT[k]
                for t in range(t0, t1):
                    at = c0 + (t - t0) * GATES
                    last = mm(bank[b][0:P, at:at + GATES], table_t[:, t * P:(t + 1) * P], whh, start=True, stop=True)
                last.then_inc(node_hidden, 1)
                pe.wait_ge(node_hidden, (ph - GRU1) * 3 + k + 1)

            def pick(ph, c, s):
                pe.wait_ge(key_hot_ready, c + (1 + (ph - GCN1) * CHUNKS))
                for j in range(CH - POOL_T[ph][s]):
                    if j % 2 == 0 and later(c, 1):
                        pe.wait_ge(picked_low, pairs_until(ph, c) + (j // 2 + 1 - PAIRS[ph]))
                    to = pick_bank[j // 2][:, (j % 2) * LOWS * FEAT:(j % 2 + 1) * LOWS * FEAT]
                    for a in range(KEYS):
                        for k in range(3):
                            last = mm(to, key_hot[s][:, a * EC + j * P:a * EC + j * P + 128], parts[:, k, a * LOWS * FEAT:(a + 1) * LOWS * FEAT],
                                      start=(a == 0 and k == 0), stop=(a == KEYS - 1 and k == 2))
                    if j % 2 == 1 or j == CH - POOL_T[ph][s] - 1:
                        last.then_inc(pick_done, pair_count(ph, s, j))

            def window_sums(ph, c, s, r, n):
                if later(c, 2):
                    pe.wait_ge(xsum_copied, c + (ph * CHUNKS - 1))
                if ph == DEG:
                    mm(sum_bank[s][0:FEAT, CW:CW + SLOTS], ones_half[:, :], onehot[:, ds(c * CH, CH), :],
                       start=True, stop=True).then_inc(summed, 1)
                    return
                pe.wait_ge(gathered[ph][r], n * (16 * POOL_T[ph][s]))
                pe.wait_ge(window_copied, c + (1 + (ph - GCN1) * CHUNKS))
                pe.wait_ge(xsrc_ready, c + (1 + (ph - GCN1) * CHUNKS))
                if ph >= GRU1:
                    pe.wait_ge(xwin_ready, c + (1 + (ph - GRU1) * CHUNKS))
                    pe.wait_ge(hidden_copied, c + (1 + (ph - GRU1) * CHUNKS))
                for j in range(CH):
                    if ph >= GRU1:
                        win = xwin[s][:, j * 128:(j + 1) * 128].rearrange("p (n i) -> p n i", i=FEAT)
                        for q in range(4):
                            mm(sum_bank[s][q * 32:(q + 1) * 32, j * 32:(j + 1) * 32],
                               hidden_ring[s][:, j * HIDDEN:(j + 1) * HIDDEN], win[:, :, q * 4:(q + 1) * 4],
                               start=True, stop=True, tile_position=(0, 32 * q))
                    last = mm(sum_bank[s][0:FEAT, CW + j * WIN:CW + (j + 1) * WIN], xsrc[r][:, j, :],
                              window[s][:, j * WIN:(j + 1) * WIN], start=True, stop=True)
                last.then_inc(summed, 1)

            def slot_sums(ph, c, s):
                pe.wait_ge(xsum_copied, c + (1 + ph * CHUNKS))
                if later(c, 1):
                    pe.wait_ge(slots_copied, c + ph * CHUNKS)
                if ph >= GRU1 and isinstance(c, int) and c == 1:
                    hidden_gates(ph, 1)
                to = slot_bank[0:SLOTS, 0:FEAT]
                if ph >= GRU1:
                    part = sums_sb[s][:, :].rearrange("p (m r) -> p r m", r=4)
                    for r in range(4):
                        mm(to, part[:, r, :], w2q[:, r, :], start=(r == 0), stop=False)
                    mm(to, xsum_sb[s][:, :], b2m[:, :], start=False, stop=True).then_inc(slotted, 1)
                else:
                    mm(to, xsum_sb[s][:, :], ident[0:FEAT, 0:FEAT], start=True, stop=True).then_inc(slotted, 1)

            def place_slots(ph, c, s):
                pe.wait_ge(slots_copied, c + (1 + ph * CHUNKS))
                pe.wait_ge(place_ready, c + (1 + ph * CHUNKS))
                if later(c, 1):
                    pe.wait_ge(added, c + ph * CHUNKS)
                if ph >= GRU1 and isinstance(c, int) and c == 1:
                    hidden_gates(ph, 2)
                mm(place_bank[0:FEAT, 0:SPAN], slots_sb[s][:, :], place[s][:, :], start=True, stop=True).then_inc(placed, 1)

            for ph in range(DEG, GRU2 + 1):
                if ph > DEG:
                    pe.wait_ge(table_ready, ph)
                    for tiles in (range(16, NT), range(16)):
                        for t in tiles:
                            last = mm(bank[t // 4][0:FEAT, (t % 4) * P:(t % 4 + 1) * P], table[:, t, :], ident[:, :],
                                      start=True, stop=True)
                        last.then_inc(table_turned, 1)
                with pe.If(general < 1):
                    def step(c, s, r, n):
                        if ph > DEG and within(c, 1):
                            pick(ph, c + 1, 1 - s)
                        window_sums(ph, c, s, r, n)
                        if ph >= GRU1 and isinstance(c, int) and c == 1:
                            hidden_gates(ph, 0)
                        if ph == DEG:
                            edge_mlp(c, s, r, n)
                        if later(c, 1):
                            slot_sums(ph, c - 1, 1 - s)
                        if later(c, 2):
                            place_slots(ph, c - 2, s)
                    if ph == GRU1:
                        pe.wait_ge(hidden_ready, CHUNKS)
                    if ph > DEG:
                        pe.wait_ge(table_t_ready, 2 * ph - 1)
                        pe.wait_ge(parts_ready, ph)
                        pick(ph, 0, 0)
                        pe.wait_ge(table_t_ready, 2 * ph)
                    steps(pe, step)
                    place_slots(ph, 73, 1)
                    slot_sums(ph, 74, 0)
                    place_slots(ph, 74, 0)
                with pe.Else():
                    if ph == DEG:
                        steps(pe, edge_mlp)
                        pe.wait_ge(hidden_ready, CHUNKS)
                    else:
                        pe.wait_ge(table_t_ready, 2 * ph)
                    with pe.Fori(0, TILES) as t:
                        if ph >= GRU1:
                            pe.wait_ge(g_prod_ready, t + (1 + (ph - GRU1) * TILES))
                            pe.wait_ge(g_hidden_copied, t + (1 + (ph - GRU1) * TILES))
                            mm(bank[7][0:HIDDEN, 256:256 + P], g_hidden, ident[:, :],
                               start=True, stop=True).then_inc(g_transposed, 1)
                            pe.wait_ge(g_hidden_ready, t + (1 + (ph - GRU1) * TILES))
                            weights = bank[7][0:P, 0:FEAT * FEAT]
                            mm(weights, g_hidden_t, w2row, start=True, stop=False).then_inc(g_weights_begun, 1)
                            pe.wait_ge(g_weights_begun, t + (1 + (ph - GRU1) * TILES))
                            mm(weights, ones[BASE:BASE + 1, :], b2row, start=False, stop=True).then_inc(g_weights, 1)
                            pe.wait_ge(g_msg_ready, t + (1 + (ph - GRU1) * TILES))
                        if ph > DEG:
                            pe.wait_ge(g_gathered[ph], t * 16 + 16)
                        what = ones[:, 0:FEAT] if ph == DEG else g_x[:, :] if ph <= GCN2 else g_msg[:, :]
                        pe.wait_ge(g_wide_ready, t + (1 + ph * TILES))
                        pe.wait_ge(g_added, t + (1 + ph * TILES))
                        for b in range(BLOCKS):
                            last = mm(bank[b][0:FEAT, 0:BLK], what, wide[:, b * BLK:(b + 1) * BLK], start=True, stop=True)
                        last.then_inc(g_blocks, 1)
                    if ph >= GRU1:
                        pe.wait_ge(g_added, 1 + (ph + 1) * TILES)
                        for k in range(3):
                            hidden_gates(ph, k)
                pe.nop()
                pe.wait_ge(node_free, ph + 1)
                if ph == DEG:
                    for t in range(NT):
                        last = mm(bank[7][0:P, t * FEAT:(t + 1) * FEAT], acc_view(t), ident[0:FEAT, 0:FEAT], start=True, stop=True)
                    last.then_inc(node_sums, 1)
                elif ph <= GCN2:
                    for t in range(NT):
                        last = mm(bank[7][0:P, t * FEAT:(t + 1) * FEAT], acc_view(t), gw[ph - GCN1][:, :], start=True, stop=True)
                    last.then_inc(node_sums, 1)
                else:
                    for b, c0, t0, t1 in INPUT_AT:
                        for t in range(t0, t1):
                            at = c0 + (t - t0) * GATES
                            last = mm(bank[b][0:P, at:at + GATES], acc_view(t), wih[:, :], start=True, stop=True)
                    last.then_inc(node_sums, 1)


def kernel(**inputs):
    import numpy as np
    import concourse.bacc as bacc
    from concourse.bass_utils import run_bass_kernel_spmd

    def flat(name, shape):
        return np.ascontiguousarray(np.asarray(inputs[name]).reshape(shape))

    def turned(name, shape):
        return np.ascontiguousarray(np.asarray(inputs[name]).reshape(shape).T)

    slot_matrix = np.concatenate([np.kron(np.eye(CH), np.ones((1, WIN))), np.tile(np.arange(WIN), (1, CH))])
    slot_matrix[0] -= 1
    edge_rows = np.zeros((2 * MLP_T * EDGE_FEAT, CHUNKS, P), np.float32)
    edge_rows[0:CH * EDGE_FEAT] = np.asarray(inputs["edge_attr_13"]).reshape(CHUNKS, CH, P, EDGE_FEAT).transpose(
        1, 3, 0, 2).reshape(CH * EDGE_FEAT, CHUNKS, P)
    arrays = {
        "x": flat("x", (NODES, FEAT)),
        "src": turned("src", (TILES, P)), "src_flat": flat("src", (P, TILES)),
        "keys": np.arange(ROWS * KEYS, dtype=np.float32).reshape(ROWS, KEYS), "dst": turned("dst", (TILES, P)),
        "first": np.ascontiguousarray(np.asarray(inputs["dst"])[::P].reshape(CHUNKS, CH).T),
        "edge_t": np.ascontiguousarray(edge_rows.reshape(2, MLP_T * EDGE_FEAT, CHUNKS, P).transpose(1, 2, 0, 3)).reshape(
            MLP_T * EDGE_FEAT, CHUNKS * 2 * P),
        "w1": flat("L1_gnn_fnet_w1", (EDGE_FEAT, HIDDEN)), "b1": flat("L1_gnn_fnet_b1", (1, HIDDEN)),
        "gw1": flat("L0_gnn_W1", (FEAT, FEAT)), "gb1": flat("L0_gnn_b1", (1, FEAT)),
        "gw2": flat("L0_gnn_W2", (FEAT, FEAT)), "gb2": flat("L0_gnn_b2", (1, FEAT)),
        "w2": flat("L1_gnn_fnet_w2", (HIDDEN, FEAT * FEAT)), "b2": flat("L1_gnn_fnet_b2", (1, FEAT * FEAT)),
        "wih_t": turned("L1_gnn_gru_w_ih", (GATES, FEAT)), "whh_t": turned("L1_gnn_gru_w_hh", (GATES, FEAT)),
        "bih": flat("L1_gnn_gru_b_ih", (1, GATES)), "bhh": flat("L1_gnn_gru_b_hh", (1, GATES)),
        "ident": np.eye(P, dtype=np.float32),
        "iota": np.tile(np.arange(BLK, dtype=np.float32), (P, 1)),
        "slot_matrix": slot_matrix.astype(np.float32),
    }
    nc = bacc.Bacc("TRN2", target_bir_lowering=False, num_devices=1)
    args = [nc.dram_tensor(f"in_{n}", a.shape, mybir.dt.from_np(a.dtype), kind="ExternalInput").ap()
            for n, a in arrays.items()]
    out = nc.dram_tensor("out", (NODES, FEAT), mybir.dt.float32, kind="ExternalOutput").ap()
    gnn_kernel(nc, *args, out)
    r = run_bass_kernel_spmd(nc, [{f"in_{n}": a for n, a in arrays.items()}], core_ids=[0])
    return r.results[0]["out"]
```
